# Optimizing a Trainium2 kernel written in Bass

```python
import numpy as np
import jax
import jax.numpy as jnp

def _softmax(x, axis=-1):
    return jax.nn.softmax(x, axis=axis)

def _gelu(x):
    return jax.nn.gelu(x, approximate=True)

def _silu(x):
    return jax.nn.silu(x)

def _sigmoid(x):
    return jax.nn.sigmoid(x)

def _layernorm(x, axis=-1, eps=1e-05):
    m = jnp.mean(x, axis=axis, keepdims=True)
    v = jnp.var(x, axis=axis, keepdims=True)
    return (x - m) / jnp.sqrt(v + eps)

def _scatter_add(tgt, idx, src, axis=0):
    return tgt.at[idx].add(src)

def _segment_sum(src, seg, n):
    return jax.ops.segment_sum(src, seg, n)
kernel_name = 'mk_adaln_d1_jaxref_r4_f67db0'

def setup_inputs(seed: int=0):
    np.random.seed(seed)
    _w = jnp.asarray

    def _L0_attn_setup():
        import jax, jax.numpy as jnp
        import numpy as np
        B, L, DM = (2, 512, 512)
        H, P, N = (32, 64, 64)
        D_INNER = H * P
        PROJ = 2 * D_INNER + 2 * H * N + H
        EPS = 1e-05
        key = jax.random.key(seed)
        k0, k1, k2 = jax.random.split(key, 3)
        return {'x': jax.random.normal(k0, (B, L, DM), jnp.float32), 'W_in': jax.random.normal(k1, (PROJ, DM), jnp.float32) * DM ** (-0.5), 'W_out': jax.random.normal(k2, (DM, D_INNER), jnp.float32) * D_INNER ** (-0.5), 'gamma': jnp.ones((D_INNER,), jnp.float32), 'beta': jnp.zeros((D_INNER,), jnp.float32), 'D': jnp.ones((H, P), jnp.float32)}
    _L0_attn_in = _L0_attn_setup()

    def _L0_ffn_setup():
        import jax, jax.numpy as jnp
        import numpy as np
        L, N, E, H, K = (512, 8, 512, 2048, 8)
        key = jax.random.key(seed)
        ks = jax.random.split(key, 6)
        return {'x': jax.random.normal(ks[0], (L, N, E), dtype=jnp.float32), 'proj1': jax.random.normal(ks[1], (H, E), dtype=jnp.float32) * 0.02, 'proj1_bias': jax.random.normal(ks[2], (H,), dtype=jnp.float32) * 0.02, 'proj2': jax.random.normal(ks[3], (E, H), dtype=jnp.float32) * 0.02, 'proj2_bias': jax.random.normal(ks[4], (E,), dtype=jnp.float32) * 0.02, 'gate_w': jax.random.normal(ks[5], (E, K), dtype=jnp.float32)}
    _L0_ffn_in = _L0_ffn_setup()
    _L0_c = _w((lambda *s: np.random.randn(*s).astype(np.float32) * 0.05)(1, 512))
    _L0_wmod = _w((lambda *s: np.random.randn(*s).astype(np.float32) * 0.05)(512, 6 * 512) * 512 ** (-0.5))
    _d = {'L0_attn_x': _L0_attn_in['x'], 'L0_attn_W_in': _L0_attn_in['W_in'], 'L0_attn_W_out': _L0_attn_in['W_out'], 'L0_attn_gamma': _L0_attn_in['gamma'], 'L0_attn_beta': _L0_attn_in['beta'], 'L0_attn_D': _L0_attn_in['D'], 'L0_ffn_proj1': _L0_ffn_in['proj1'], 'L0_ffn_proj1_bias': _L0_ffn_in['proj1_bias'], 'L0_ffn_proj2': _L0_ffn_in['proj2'], 'L0_ffn_proj2_bias': _L0_ffn_in['proj2_bias'], 'L0_ffn_gate_w': _L0_ffn_in['gate_w'], 'L0_c': _L0_c, 'L0_wmod': _L0_wmod}
    _x0 = _d['L0_attn_x']
    _d['L0_attn_x'] = jax.random.normal(jax.random.fold_in(jax.random.key(seed), 1), (1, 2048, 512), dtype=_x0.dtype)
    del _x0
    return _d

def reference(L0_attn_x, L0_attn_W_in, L0_attn_W_out, L0_attn_gamma, L0_attn_beta, L0_attn_D, L0_ffn_proj1, L0_ffn_proj1_bias, L0_ffn_proj2, L0_ffn_proj2_bias, L0_ffn_gate_w, L0_c, L0_wmod):

    def _L0_attn_ref(x, W_in, W_out, gamma, beta, D):
        import jax, jax.numpy as jnp
        import numpy as np
        B, L, DM = (2, 512, 512)
        H, P, N = (32, 64, 64)
        D_INNER = H * P
        PROJ = 2 * D_INNER + 2 * H * N + H
        EPS = 1e-05
        Bz, Lz, _ = x.shape
        zxbca = x @ W_in.T
        x_t, z_t, b_t, c_t, a_log = jnp.split(zxbca, [D_INNER, 2 * D_INNER, 2 * D_INNER + H * N, 2 * D_INNER + 2 * H * N], axis=-1)
        x_t = x_t.reshape(Bz, Lz, H, P)
        b_t = b_t.reshape(Bz, Lz, H, N)
        c_t = c_t.reshape(Bz, Lz, H, N)
        decay = jnp.exp(-jnp.exp(a_log))

        def step(states, inp):
            xt, bt, ct, dec = inp
            states = states * dec[:, :, None, None] + xt[..., None] * bt[:, :, None, :]
            yt = jnp.einsum('bhpn,bhn->bhp', states, ct) + xt * D
            return (states, yt)
        init = jnp.zeros((Bz, H, P, N), x.dtype)
        xs = (jnp.moveaxis(x_t, 1, 0), jnp.moveaxis(b_t, 1, 0), jnp.moveaxis(c_t, 1, 0), jnp.moveaxis(decay, 1, 0))
        _, ys = jax.lax.scan(step, init, xs)
        y = jnp.moveaxis(ys, 0, 1).reshape(Bz, Lz, D_INNER)
        y = y * jax.nn.silu(z_t)
        mu = y.mean(-1, keepdims=True)
        var = y.var(-1, keepdims=True)
        y = (y - mu) * jax.lax.rsqrt(var + EPS) * gamma + beta
        return y @ W_out.T

    def _L0_ffn_ref(x, proj1, proj1_bias, proj2, proj2_bias, gate_w):
        import jax, jax.numpy as jnp
        import numpy as np
        L, N, E, H, K = (512, 8, 512, 2048, 8)
        dst = jnp.argmax(jnp.einsum('lne,ek->lnk', x, gate_w), axis=-1)
        h = jax.nn.gelu(jnp.einsum('lne,he->lnh', x, proj1) + proj1_bias, approximate=False)
        out = jnp.einsum('lnh,eh->lne', h, proj2) + proj2_bias
        del dst
        return out
    x = L0_attn_x
    mod = (_silu(L0_c) @ L0_wmod).reshape(L0_c.shape[0], 6, 1, -1)
    sa, ca, ga, sb, cb, gb = (mod[:, 0], mod[:, 1], mod[:, 2], mod[:, 3], mod[:, 4], mod[:, 5])
    ga = (2 * (ga >= 0) - 1) * jnp.maximum(jnp.abs(ga), 0.25)
    gb = (2 * (gb >= 0) - 1) * jnp.maximum(jnp.abs(gb), 0.25)
    h = _layernorm(x, axis=-1) * (1 + ca) + sa
    x = x + ga * _L0_attn_ref(h, L0_attn_W_in, L0_attn_W_out, L0_attn_gamma, L0_attn_beta, L0_attn_D)
    h = _layernorm(x, axis=-1) * (1 + cb) + sb
    x = x + gb * _L0_ffn_ref(h, L0_ffn_proj1, L0_ffn_proj1_bias, L0_ffn_proj2, L0_ffn_proj2_bias, L0_ffn_gate_w)
    return x

_drawn_inputs = setup_inputs


def setup_inputs(seed=0):
    import zlib

    import numpy as np

    out = dict(_drawn_inputs(seed))
    spreads = {'L0_attn_gamma': (1.0, 0.2), 'L0_attn_beta': (0.0, 0.327), 'L0_attn_D': (1.0, 0.6)}
    factors = {'L0_ffn_proj1_bias': 8.0, 'L0_ffn_proj2_bias': 8.0}
    for name, (base, spread) in spreads.items():
        noise = np.random.default_rng([zlib.crc32(name.encode()), seed]).standard_normal(out[name].shape)
        drawn = base * np.exp(spread * noise) if base else spread * noise
        out[name] = jnp.asarray(drawn.astype(out[name].dtype))
    for name, factor in factors.items():
        out[name] = (out[name] * factor).astype(out[name].dtype)
    return out
```

```python
from contextlib import ExitStack

import concourse.bass as bass
from concourse import mybir

ALU = mybir.AluOpType
ACT = mybir.ActivationFunctionType
F32 = mybir.dt.float32
F32R = mybir.dt.float32r
BF16 = mybir.dt.bfloat16

P = 128
TOKENS = 2048
E = 512
KT = E // P
HEADS = 32
HD = 64
INNER = HEADS * HD
PAIRS = INNER // P
SUP = 512
CH = SUP // P
NS = TOKENS // SUP
NT = TOKENS // P
HID = 2048
HG = HID // P
EPS = 1e-5
NEG = -1e30
B_, C_, X_, Z_, O_ = range(5)


def adaln_block(nc, x, w_pairs, w_decay, w_out, gamma, beta, skip, w1, b1, w2, b2, cond, w_mod, out):
    crows = nc.dram_tensor("cum_rows_scratch", (HEADS, 3, TOKENS), BF16, kind="Internal").ap()

    with ExitStack() as ctx:
        def sb(name, shape, dt=F32):
            return ctx.enter_context(nc.sbuf_tensor(name, shape, dt))

        def sem(name):
            return ctx.enter_context(nc.semaphore(name))

        ps = [ctx.enter_context(nc.psum_tensor(f"bank{i}", [P, 512], F32)) for i in range(8)]

        hT_hi = sb("hT_hi", [P, KT, TOKENS], F32R)
        hT_lo = sb("hT_lo", [P, KT, TOKENS], F32R)
        acc = sb("acc", [P, NT, E])
        y_sum = sb("y_sum", [P, TOKENS])
        yy_sum = sb("yy_sum", [P, TOKENS])
        raw = [sb(f"raw{m}", [P, 512]) for m in range(5)]
        w_hi = [sb(f"w_hi{m}", [P, 512], F32R) for m in range(5)]
        w_lo = [sb(f"w_lo{m}", [P, 512], F32R) for m in range(5)]
        w_scaled = sb("w_scaled", [P, E])
        wg_sum = sb("wg_sum", [P, E])
        wb_sum = sb("wb_sum", [P, E])
        bT = sb("bT", [P, SUP])
        cT = sb("cT", [P, SUP])
        xT = sb("xT", [P, SUP])
        gate = sb("gate", [P, SUP])
        x_tok = sb("x_tok", [P, CH, P])
        b_tok = sb("b_tok", [P, CH, P])
        dec = sb("dec", [P, 2, SUP])
        e_cum = sb("e_cum", [P, SUP])
        c_dec = sb("c_dec", [P, SUP])
        state = sb("state", [P, 8, P])
        y_raw = sb("y_raw", [P, SUP])
        y_sq = sb("y_sq", [P, SUP])
        y_hi = sb("y_hi", [P, 2, SUP], F32R)
        y_lo = sb("y_lo", [P, 2, SUP], F32R)
        rows = [sb(f"rows{i}", [6, SUP], BF16) for i in range(2)]
        xin = sb("xin", [P, CH, E])
        gate_a = sb("gate_a", [P, E])
        gate_b = sb("gate_b", [P, E])
        gb_b2 = sb("gb_b2", [P, E])
        ncum = sb("ncum", [P, NT, HEADS])
        w_end = sb("w_end", [P, NT, HEADS])
        ncum_pair = sb("ncum_pair", [P, NT, 2])
        b1_pair = sb("b1_pair", [P, 2])
        ident = sb("ident", [P, P])
        ident_b = sb("ident_b", [P, P], BF16)
        causal = sb("causal", [P, P], BF16)
        sel = sb("sel", [6, 3, P], BF16)
        ones = sb("ones", [P, P])
        pick0 = sb("pick0", [P, 2])
        mean_w = sb("mean_w", [P, 2])
        mod_col = sb("mod_col", [P, 16, 2])
        gamma_c = sb("gamma_c", [P, PAIRS])
        beta_c = sb("beta_c", [P, PAIRS])
        skip_c = sb("skip_c", [P, PAIRS])
        b1_c = sb("b1_c", [P, HG])
        cc = sb("cc", [P, 4, KT])
        bst = sb("bst", [P, CH, 6])
        mv = sb("mv", [P, CH, 2])
        rs = sb("rs", [P, 4, NT])
        yst = sb("yst", [P, NT, 4])
        yv = sb("yv", [P, 3, NT])
        wa = w_scaled[:, 0:KT * HEADS].rearrange("p (k h) -> p k h", k=KT)
        w_mod_sb = acc[:, :, :].rearrange("p (j k) e -> p j k e", j=4)
        silu_b = dec[:, 0, :].rearrange("p (k m) -> p k m", k=KT)
        mod_row = [bT, cT, xT, x_tok[:, :, :].rearrange("p c m -> p (c m)")]
        h_raw = [y_raw, y_sq]
        ea = gate[0:HEADS, :]
        cum_r = e_cum[0:HEADS, :]
        wend_r = c_dec[0:HEADS, :]
        rest = b_tok[0:HEADS, :, :].rearrange("p c m -> p (c m)")
        parts = dec[0:HEADS, :, :].rearrange("p a n -> p (a n)").bitcast(BF16)[:, 0:3 * SUP]\
            .rearrange("p (j n) -> p j n", j=3)
        s1_row, beta_row = bT, cT
        b2_row = x_tok[:, :, :].rearrange("p c m -> p (c m)")

        const_loaded = sem("const_loaded")
        cond_loaded = sem("cond_loaded")
        wmod_loaded = [sem(f"wmod_loaded{i}") for i in range(4)]
        x_loaded = sem("x_loaded")
        raw_loaded = [sem(f"raw_loaded{m}") for m in range(5)]
        rows_loaded = [sem(f"rows_loaded{i}") for i in range(2)]
        crows_stored = sem("crows_stored")
        out_stored = sem("out_stored")
        consts_made = sem("consts_made")
        silu_exp = sem("silu_exp")
        silu_ready = sem("silu_ready")
        mod_psum = sem("mod_psum")
        mod_ready = sem("mod_ready")
        modcol_psum = sem("modcol_psum")
        modcol_ready = sem("modcol_ready")
        dve_chain = sem("dve_chain")
        pool_chain = sem("pool_chain")
        var_ready = sem("var_ready")
        std_ready = sem("std_ready")
        xn_ready = sem("xn_ready")
        xnT_psum = sem("xnT_psum")
        hraw_ready = sem("hraw_ready")
        hhi_ready = sem("hhi_ready")
        hlo_ready = sem("hlo_ready")
        ea_ready = sem("ea_ready")
        cum_ready = sem("cum_ready")
        wend_arg = sem("wend_arg")
        wend_ready = sem("wend_ready")
        parts_ready = sem("parts_ready")
        cols_psum = sem("cols_psum")
        cols_ready = sem("cols_ready")
        whi_ready = [sem(f"whi_ready{m}") for m in range(5)]
        wlo_ready = [sem(f"wlo_ready{m}") for m in range(5)]
        wscaled_ready = sem("wscaled_ready")
        bT_psum, cT_psum, xT_psum, zT_psum = (sem(f"{n}T_psum") for n in "bcxz")
        bT_ready, cT_ready, xT_ready, tanh_ready = (sem(f"{n}_ready") for n in ("bT", "cT", "xT", "tanh"))
        gate_ready = sem("gate_ready")
        xtok_psum, btok_psum = sem("xtok_psum"), sem("btok_psum")
        xtok_ready, btok_ready = sem("xtok_ready"), sem("btok_ready")
        scores_psum = sem("scores_psum")
        decay_psum = sem("decay_psum")
        decay_ready = sem("decay_ready")
        ecum_ready = sem("ecum_ready")
        cdec_ready = sem("cdec_ready")
        mixed_ready = sem("mixed_ready")
        dstate_psum = sem("dstate_psum")
        state_step = sem("state_step")
        y_psum = sem("y_psum")
        y_skip = sem("y_skip")
        y_ready = sem("y_ready")
        yhi_ready = sem("yhi_ready")
        ylo_ready = sem("ylo_ready")
        ystats_done = sem("ystats_done")
        out_psum = sem("out_psum")
        acc_added = sem("acc_added")
        wsums_ready = sem("wsums_ready")
        norm_psum = sem("norm_psum")
        xb_ready = sem("xb_ready")
        x1_ready = sem("x1_ready")
        acc_set = sem("acc_set")
        w2_scaled = sem("w2_scaled")
        hid_psum = sem("hid_psum")
        gelu_ready = sem("gelu_ready")
        ghi_ready = sem("ghi_ready")
        glo_ready = sem("glo_ready")
        mlp_psum = sem("mlp_psum")
        mlp_added = sem("mlp_added")
        wsums_step = sem("wsums_step")
        ncum_pair_ready = sem("ncum_pair_ready")
        b1_ready = sem("b1_ready")
        wsums_scaled = sem("wsums_scaled")
        a_psum = sem("a_psum")

        def wait(eng, s, value):
            if not (isinstance(value, int) and value <= 0):
                eng.wait_ge(s, value)

        def after(g, s):
            return (g, s + 1) if s + 1 < NS else (g + 1, 0)

        def mixer(eng, step):
            step(None, (0, 0))
            for s in range(NS):
                step((0, s), after(0, s))
            with eng.Fori(1, PAIRS - 1) as g:
                for s in range(NS):
                    step((g, s), after(g, s))
            for s in range(NS):
                step((PAIRS - 1, s), after(PAIRS - 1, s) if s + 1 < NS else None)

        def mlp(eng, step):
            def pair(g0, last):
                for j in range(2):
                    for s in range(NS):
                        end = last and j == 1 and s + 1 == NS
                        nxt = (g0 + j, s + 1, j) if s + 1 < NS else (g0 + j + 1, 0, 1 - j)
                        step((g0 + j, s, j), None if end else nxt)
            step(None, (0, 0, 0))
            pair(0, False)
            with eng.Fori(1, HG // 2 - 1) as r:
                pair(r * 2, False)
            pair(HG - 2, True)

        def split_count(g, j):
            return PAIRS + (g - j) // 2 + 1

        x_rows = x.rearrange("(s c p) e -> s p c e", p=P, c=CH)
        out_rows = out.rearrange("(s c p) e -> s p c e", p=P, c=CH)

        block = ctx.enter_context(nc.Block())

        @block.sync
        def _(sp):
            sp.dma_start(cc[:, 0, :], cond).then_inc(cond_loaded, 16)
            for j in range(4):
                sp.dma_start(w_mod_sb[:, j], w_mod[j]).then_inc(wmod_loaded[j], 16)
            sp.dma_start(xin[:], x_rows[0]).then_inc(x_loaded, 16)
            for dst, src in ((gamma_c, gamma), (beta_c, beta), (skip_c, skip), (b1_c, b1)):
                sp.dma_start(dst[:], src).then_inc(const_loaded, 16)
            sp.dma_start(wa, w_decay).then_inc(const_loaded, 16)
            for j in (4, 5):
                sp.wait_ge(mod_psum, j - 3)
                sp.dma_start(w_mod_sb[:, j - 4], w_mod[j]).then_inc(wmod_loaded[j - 4], 16)
            sp.wait_ge(modcol_psum, 1)
            sp.dma_start(b2_row, b2.partition_broadcast(P)).then_inc(const_loaded, 16)
            for m in range(5):
                sp.dma_start(raw[m][:], w_pairs[0, m] if m < O_ else w_out[0]).then_inc(raw_loaded[m], 16)
            for s in range(NS):
                sp.wait_ge(parts_ready, s + 1)
                sp.dma_start(crows[:, :, s * SUP:(s + 1) * SUP], parts).then_inc(crows_stored, 16)
                if s + 1 < NS:
                    sp.wait_ge(xnT_psum, KT * (s + 1))
                    sp.dma_start(xin[:], x_rows[s + 1]).then_inc(x_loaded, 16)
            sp.wait_ge(crows_stored, 16 * NS)

            def step(cur, nxt):
                if nxt:
                    g, s = nxt
                    wait(sp, decay_psum, 3 * (NS * g + s - 1))
                    src = crows[bass.ds(2 * g, 2), :, s * SUP:(s + 1) * SUP].rearrange("a j n -> (a j) n")
                    sp.dma_start(rows[s % 2][:], src).then_inc(rows_loaded[s % 2], 16)
                if cur and cur[1] == 0 and not (isinstance(cur[0], int) and cur[0] + 1 >= PAIRS):
                    g = cur[0] + 1
                    for m in range(5):
                        sp.wait_ge(wlo_ready[m] if m < O_ else wscaled_ready, g)
                        src = w_pairs[bass.ds(g, 1), m] if m < O_ else w_out[bass.ds(g, 1)]
                        sp.dma_start(raw[m][:], src.rearrange("a p n -> (a p) n"))\
                            .then_inc(raw_loaded[m], 16)
            mixer(sp, step)

            for s in range(NS):
                wait(sp, xnT_psum, KT * (NS + s))
                sp.dma_start(xin[:], x_rows[s]).then_inc(x_loaded, 16)
                if s == 0:
                    for g in range(2):
                        sp.wait_ge(wlo_ready[g], PAIRS)
                        sp.dma_start(raw[g][:], w1[g]).then_inc(raw_loaded[g], 16)
                        sp.wait_ge(wlo_ready[2 + g], PAIRS)
                        sp.dma_start(raw[2 + g][:], w2[g]).then_inc(raw_loaded[2 + g], 16)

            def mlp_step(cur, nxt):
                if cur and cur[1] == 0 and not (isinstance(cur[0], int) and cur[0] + 2 >= HG):
                    g, _, j = cur
                    gn = g + 2
                    for m, src in ((j, w1), (2 + j, w2)):
                        sp.wait_ge(wlo_ready[m], split_count(g, j))
                        sp.dma_start(raw[m][:], src[bass.ds(gn, 1)].rearrange("a p n -> (a p) n"))\
                            .then_inc(raw_loaded[m], 16)
                if cur and isinstance(cur[0], int) and cur[0] == HG - 1:
                    s = cur[1]
                    sp.wait_ge(mlp_added, CH * (NS * cur[0] + s + 1))
                    sp.dma_start(out_rows[s], acc[:, CH * s:CH * (s + 1), :]).then_inc(out_stored, 16)
            mlp(sp, mlp_step)
            sp.wait_ge(out_stored, 16 * NS)

        @block.gpsimd
        def _(pool):
            for t, value in ((ident, 0.0), (ident_b, 0.0), (causal, 0.0), (sel, 1.0), (ones, 1.0),
                             (pick0, 0.0), (mean_w, 1.0 / INNER), (wg_sum, 0.0), (wb_sum, 0.0),
                             (y_sum, 0.0), (yy_sum, 0.0), (state, 0.0)):
                nc.gpsimd.memset(t[:], value).then_inc(pool_chain, 1)
            pool.wait_ge(pool_chain, 12)
            for m in (ident, ident_b):
                nc.gpsimd.affine_select(out=m[:], in_=m[:], compare_op=ALU.not_equal, fill=1.0, base=0,
                                        pattern=[[-1, P]], channel_multiplier=1).then_inc(consts_made, 1)
            nc.gpsimd.affine_select(out=causal[:], in_=causal[:], compare_op=ALU.is_ge, fill=NEG, base=0,
                                    pattern=[[1, P]], channel_multiplier=-1).then_inc(consts_made, 1)
            first = dict(compare_op=ALU.is_ge, fill=0.0, base=2, channel_multiplier=-1)
            second = dict(compare_op=ALU.is_ge, fill=0.0, base=-3, channel_multiplier=1)
            for view, n, which in ((sel[:, 0, :], P, first), (sel[:, 1, :], P, second),
                                   (sel[:, 2, 0:HD], HD, first), (sel[:, 2, HD:P], HD, second)):
                nc.gpsimd.affine_select(out=view, in_=view, pattern=[[0, n]], **which)\
                    .then_inc(consts_made, 1)
            nc.gpsimd.memset(pick0[0:1, :], 1.0).then_inc(consts_made, 1)

            def hT_low(i, s, k):
                pool.wait_ge(hraw_ready, i)
                pool.wait_ge(hhi_ready, i)
                hi = hT_hi[:, k, s * SUP:(s + 1) * SUP].bitcast(F32)
                nc.gpsimd.tensor_tensor(hT_lo[:, k, s * SUP:(s + 1) * SUP], h_raw[k % 2][:], hi,
                                        ALU.subtract).then_inc(hlo_ready, 1)

            for s in range(NS):
                for k in range(KT):
                    hT_low(KT * s + k + 1, s, k)

            def split_low(m, source, count):
                pool.wait_ge(whi_ready[m], count)
                nc.gpsimd.tensor_tensor(w_lo[m][:], source[:], w_hi[m][:].bitcast(F32), ALU.subtract)\
                    .then_inc(wlo_ready[m], 1)

            for m in range(5):
                split_low(m, raw[m] if m < O_ else w_scaled, 1)

            def step(cur, nxt):
                more = nxt and nxt[1] == NS - 1 and not (isinstance(nxt[0], int) and nxt[0] + 1 >= PAIRS)
                if cur:
                    g, s = cur
                    u = NS * g + s
                    pool.wait_ge(ecum_ready, u + 1)
                    pool.wait_ge(cT_ready, u + 1)
                    nc.gpsimd.tensor_tensor(c_dec[:], cT[:], e_cum[:], ALU.mult).then_inc(cdec_ready, 1)
                    if s == 0 and not (isinstance(g, int) and g == 0):
                        split_low(O_, w_scaled, g + 1)
                if more:
                    split_low(B_, raw[B_], nxt[0] + 2)
                    split_low(C_, raw[C_], nxt[0] + 2)
                if cur:
                    pool.wait_ge(y_ready, u + 1)
                    tokens = slice(s * SUP, (s + 1) * SUP)
                    wait(pool, ystats_done, 2 * u)
                    nc.gpsimd.tensor_tensor(y_sq[:], y_raw[:], y_raw[:], ALU.mult).then_inc(pool_chain, 1)
                    pool.wait_ge(yhi_ready, u + 1)
                    nc.gpsimd.tensor_tensor(y_lo[:, 0, :], y_raw[:], y_hi[:, 0, :].bitcast(F32),
                                            ALU.subtract).then_inc(ylo_ready, 1)
                    nc.gpsimd.tensor_tensor(y_sum[:, tokens], y_sum[:, tokens], y_raw[:], ALU.add)\
                        .then_inc(ystats_done, 1)
                    pool.wait_ge(pool_chain, 13 + u)
                    nc.gpsimd.tensor_tensor(yy_sum[:, tokens], yy_sum[:, tokens], y_sq[:], ALU.add)\
                        .then_inc(ystats_done, 1)
                if more:
                    split_low(X_, raw[X_], nxt[0] + 2)
                    split_low(Z_, raw[Z_], nxt[0] + 2)
            mixer(pool, step)

            for s in range(NS):
                pool.wait_ge(x_loaded, 16 * (NS + s + 1))
                pool.wait_ge(wsums_ready, 2)
                for c in range(CH):
                    nc.gpsimd.tensor_tensor(xin[:, c, :], xin[:, c, :], beta_row[:], ALU.add)\
                        .then_inc(xb_ready, 1)
                for c in range(CH):
                    pool.wait_ge(x1_ready, CH * s + c + 1)
                    nc.gpsimd.tensor_tensor(acc[:, CH * s + c, :], xin[:, c, :], gb_b2[:], ALU.add)\
                        .then_inc(acc_set, 1)
                for k in range(KT):
                    hT_low(KT * (NS + s) + k + 1, s, k)

            def mlp_split(g, j):
                count = split_count(g, j)
                split_low(j, raw[j], count)
                split_low(2 + j, raw[2 + j], count)
            for g in range(2):
                mlp_split(g, g)

            def mlp_step(cur, nxt):
                if nxt:
                    g, s, j = nxt
                    v = NS * g + s
                    pool.wait_ge(gelu_ready, v + 1)
                    pool.wait_ge(ghi_ready, v + 1)
                    nc.gpsimd.tensor_tensor(y_lo[:, s % 2, :], h_raw[s % 2][:], y_hi[:, s % 2, :].bitcast(F32),
                                            ALU.subtract).then_inc(glo_ready, 1)
                if cur and cur[1] == NS - 1 and not (isinstance(cur[0], int) and cur[0] + 2 >= HG):
                    mlp_split(cur[0] + 2, cur[2])
            mlp(pool, mlp_step)

        @block.scalar
        def _(act):
            act.wait_ge(cond_loaded, 16)
            nc.scalar.activation(cc[:, 1, :], cc[:, 0, :], ACT.Exp, scale=-1.0).then_inc(silu_exp, 1)

            def hT_high(i, s, k):
                act.wait_ge(hraw_ready, i)
                nc.scalar.copy(hT_hi[:, k, s * SUP:(s + 1) * SUP], h_raw[k % 2][:]).then_inc(hhi_ready, 1)

            for s in range(NS):
                act.wait_ge(var_ready, s + 1)
                nc.scalar.activation(rs[:, 1, 0:CH], rs[:, 0, 0:CH], ACT.Sqrt).then_inc(std_ready, 1)
                for k in range(KT):
                    hT_high(KT * s + k + 1, s, k)
                act.wait_ge(a_psum, KT * (s + 1))
                nc.scalar.activation(ea, ps[0][0:HEADS, :], ACT.Exp).then_inc(ea_ready, 1)
                act.wait_ge(wend_arg, s + 1)
                nc.scalar.activation(wend_r, wend_r, ACT.Exp, scale=-1.0).then_inc(wend_ready, 1)

            def split_high(m, source):
                nc.scalar.copy(w_hi[m][:], source[:]).then_inc(whi_ready[m], 1)

            for m in range(4):
                act.wait_ge(raw_loaded[m], 16)
                split_high(m, raw[m])
            act.wait_ge(wscaled_ready, 1)
            split_high(O_, w_scaled)

            def step(cur, nxt):
                more = nxt and nxt[1] == NS - 1 and not (isinstance(nxt[0], int) and nxt[0] + 1 >= PAIRS)

                def next_weights(m):
                    if more:
                        act.wait_ge(raw_loaded[m], 16 * (nxt[0] + 2))
                        split_high(m, raw[m])

                if cur:
                    g, s = cur
                    u = NS * g + s
                    act.wait_ge(xtok_psum, u + 1)
                    nc.scalar.copy(x_tok[:].rearrange("p c m -> p (c m)"), ps[4][:]).then_inc(xtok_ready, 1)
                    if s == 0 and not (isinstance(g, int) and g == 0):
                        act.wait_ge(wscaled_ready, g + 1)
                        act.wait_ge(out_psum, CH * u)
                        split_high(O_, w_scaled)
                if nxt:
                    gn, sn = nxt
                    n = NS * gn + sn
                    act.wait_ge(bT_psum, n + 1)
                    nc.scalar.copy(bT[:], ps[0][:]).then_inc(bT_ready, 1)
                    next_weights(B_)
                    act.wait_ge(cT_psum, n + 1)
                    wait(act, cdec_ready, n)
                    nc.scalar.copy(cT[:], ps[1][:]).then_inc(cT_ready, 1)
                    next_weights(C_)
                if cur:
                    act.wait_ge(y_ready, u + 1)
                    nc.scalar.copy(y_hi[:, 0, :], y_raw[:]).then_inc(yhi_ready, 1)
                if nxt:
                    act.wait_ge(xT_psum, n + 1)
                    wait(act, y_skip, n)
                    nc.scalar.copy(xT[:], ps[0][:]).then_inc(xT_ready, 1)
                    next_weights(X_)
                    if sn == 0:
                        act.wait_ge(ncum_pair_ready, gn + 1)
                    for a in range(2):
                        act.wait_ge(decay_psum, 3 * n + a + 1)
                        for c in range(CH):
                            part = slice(c * P, (c + 1) * P)
                            ins = nc.scalar.activation(dec[:, a, part], ps[2 + a][:, part], ACT.Exp,
                                                       bias=ncum_pair[:, CH * sn + c, a:a + 1])
                        ins.then_inc(decay_ready, 1)
                    act.wait_ge(decay_psum, 3 * n + 3)
                    nc.scalar.activation(e_cum[:], ps[4][:], ACT.Exp).then_inc(ecum_ready, 1)
                    act.wait_ge(zT_psum, n + 1)
                    wait(act, y_ready, n)
                    nc.scalar.activation(gate[:], ps[1][:], ACT.Tanh, scale=0.5).then_inc(tanh_ready, 1)
                    next_weights(Z_)
            mixer(act, step)

            act.wait_ge(var_ready, NS + 1)
            nc.scalar.activation(yv[:, 1, :], yv[:, 0, :], ACT.Sqrt).then_inc(std_ready, 1)
            for s in range(NS):
                act.wait_ge(var_ready, NS + s + 2)
                nc.scalar.activation(rs[:, 1, 0:CH], rs[:, 0, 0:CH], ACT.Sqrt).then_inc(std_ready, 1)
                for k in range(KT):
                    hT_high(KT * (NS + s) + k + 1, s, k)

            def mlp_split(g, j):
                act.wait_ge(raw_loaded[j], 16 * split_count(g, j))
                split_high(j, raw[j])
                act.wait_ge(w2_scaled, g + 1)
                split_high(2 + j, raw[2 + j])
            for g in range(2):
                mlp_split(g, g)

            def mlp_step(cur, nxt):
                if nxt:
                    g, s, j = nxt
                    v = NS * g + s
                    act.wait_ge(hid_psum, v + 1)
                    if s == 0:
                        act.wait_ge(b1_ready, g + 1)
                    wait(act, glo_ready, v - 1)
                    nc.scalar.activation(h_raw[s % 2][:], ps[s % 2][:], ACT.Gelu, bias=b1_pair[:, j:j + 1])\
                        .then_inc(gelu_ready, 1)
                    wait(act, mlp_psum, CH * (v - 1))
                    act.wait_ge(gelu_ready, v + 1)
                    nc.scalar.copy(y_hi[:, s % 2, :], h_raw[s % 2][:]).then_inc(ghi_ready, 1)
                if cur and cur[1] == NS - 1 and not (isinstance(cur[0], int) and cur[0] + 2 >= HG):
                    act.wait_ge(mlp_psum, CH * (NS * cur[0] + NS))
                    mlp_split(cur[0] + 2, cur[2])
            mlp(act, mlp_step)

        @block.vector
        def _(dve):
            chain = [0]

            def link(ins):
                chain[0] += 1
                ins.then_inc(dve_chain, 1)
                dve.wait_ge(dve_chain, chain[0])

            dve.wait_ge(silu_exp, 1)
            link(nc.vector.tensor_scalar(cc[:, 1, :], cc[:, 1, :], 1.0, None, ALU.add))
            link(nc.vector.reciprocal(cc[:, 2, :], cc[:, 1, :]))
            link(nc.vector.tensor_tensor(cc[:, 3, :], cc[:, 0, :], cc[:, 2, :], ALU.mult))
            dve.wait_ge(pool_chain, 12)
            for k in range(KT):
                nc.vector.tensor_scalar(silu_b[:, k, :], ones[:], cc[:, 3, k:k + 1], None, ALU.mult)\
                    .then_inc(silu_ready, 1)

            for j in range(6):
                dve.wait_ge(mod_psum, j + 1)
                bank = ps[6 + j % 2]
                if j in (2, 5):
                    dst, sign = (gate_a if j == 2 else gate_b), y_raw
                    link(nc.vector.tensor_scalar(sign[:], bank[:], 0.0, 2.0, ALU.is_ge, ALU.mult))
                    link(nc.vector.tensor_scalar(sign[:], sign[:], -1.0, None, ALU.add))
                    nc.vector.tensor_tensor(dst[:], sign[:], bank[:], ALU.mult).then_inc(mod_ready, 1)
                    dve.wait_ge(mod_ready, j + 1)
                    link(nc.vector.scalar_tensor_tensor(dst[:], dst[:], 0.25, sign[:], ALU.max, ALU.mult))
                else:
                    nc.vector.tensor_scalar(mod_row[(j if j < 2 else j - 1)][:], bank[:],
                                            float(j in (1, 4)), None, ALU.add).then_inc(mod_ready, 1)
            dve.wait_ge(modcol_psum, 1)
            nc.vector.tensor_copy(mod_col[:], ps[1][:, 0:32].rearrange("p (v n) -> p v n", n=2))\
                .then_inc(modcol_ready, 1)
            dve.wait_ge(const_loaded, 16 * 6)
            nc.vector.tensor_tensor(gb_b2[:], gate_b[:], b2_row, ALU.mult).then_inc(modcol_ready, 1)

            def rsqrt(var, std, r, t, count):
                dve.wait_ge(std_ready, count)
                link(nc.vector.reciprocal(r, std))
                link(nc.vector.tensor_tensor(t, r, r, ALU.mult))
                link(nc.vector.tensor_tensor(t, t, var, ALU.mult))
                link(nc.vector.tensor_scalar(t, t, -0.5, 1.5, ALU.mult, ALU.add))
                link(nc.vector.tensor_tensor(r, r, t, ALU.mult))

            def norm_rows(i, var_count):
                for c in range(CH):
                    link(nc.vector.bn_stats(bst[:, c, :], xin[:, c, :]))
                    link(nc.vector.bn_aggr(mv[:, c, :], bst[:, c, :]))
                nc.vector.tensor_scalar(rs[:, 0, 0:CH], mv[:, :, 1], EPS, None, ALU.add)\
                    .then_inc(var_ready, 1)
                dve.wait_ge(var_ready, var_count)
                rsqrt(rs[:, 0, 0:CH], rs[:, 1, 0:CH], rs[:, 2, 0:CH], rs[:, 3, 0:CH], var_count)
                wait(dve, acc_set, CH * (i - NS + 1))
                for c in range(CH):
                    nc.vector.tensor_scalar(xin[:, c, :], xin[:, c, :], mv[:, c, 0:1], rs[:, 2, c:c + 1],
                                            ALU.subtract, ALU.mult).then_inc(xn_ready, 1)

            def modulate(i, s, vec):
                for k in range(KT):
                    n = KT * i + k + 1
                    dve.wait_ge(xnT_psum, n)
                    wait(dve, hlo_ready, n - 2)
                    if i < NS:
                        wait(dve, a_psum, n - 2)
                    nc.vector.tensor_scalar(h_raw[k % 2][:], ps[2 + k][:], mod_col[:, vec + 4 + k, 0:1],
                                            mod_col[:, vec + k, 0:1], ALU.mult, ALU.add)\
                        .then_inc(hraw_ready, 1)

            dve.wait_ge(modcol_ready, 2)
            for s in range(NS):
                dve.wait_ge(x_loaded, 16 * (s + 1))
                norm_rows(s, s + 1)
                modulate(s, s, 0)
                dve.wait_ge(ea_ready, s + 1)
                if s:
                    dve.wait_ge(cols_psum, s)
                    dve.wait_ge(crows_stored, 16 * s)
                for c in range(CH):
                    part = slice(c * P, (c + 1) * P)
                    nc.vector.tensor_tensor_scan(cum_r[:, part], ones[0:HEADS, :], ea[:, part], 0.0,
                                                 ALU.mult, ALU.subtract).then_inc(cum_ready, 1)
                dve.wait_ge(cum_ready, CH * (s + 1))
                for c in range(CH):
                    part, last = slice(c * P, (c + 1) * P), (c + 1) * P - 1
                    ins = nc.vector.tensor_scalar(wend_r[:, part], cum_r[:, part], cum_r[:, last:last + 1],
                                                  None, ALU.subtract)
                ins.then_inc(wend_arg, 1)
                link(nc.vector.tensor_copy(parts[:, 0, :], cum_r))
                link(nc.vector.tensor_tensor(rest, cum_r, parts[:, 0, :], ALU.subtract))
                link(nc.vector.tensor_copy(parts[:, 1, :], rest))
                nc.vector.tensor_tensor(parts[:, 2, :], rest, parts[:, 1, :], ALU.subtract)\
                    .then_inc(parts_ready, 1)
                dve.wait_ge(cols_psum, s + 1)
                nc.vector.tensor_scalar(ncum[:, CH * s:CH * (s + 1), :],
                                        ps[1][:, 0:P].rearrange("p (c h) -> p c h", c=CH), -1.0, None,
                                        ALU.mult).then_inc(cols_ready, 1)
                nc.vector.tensor_copy(w_end[:, CH * s:CH * (s + 1), :],
                                      ps[1][:, P:2 * P].rearrange("p (c h) -> p c h", c=CH))\
                    .then_inc(cols_ready, 1)

            def scale_output_weights(g):
                gm, bt = gamma_c[:, bass.ds(g, 1)], beta_c[:, bass.ds(g, 1)]
                dve.wait_ge(raw_loaded[O_], 16 * (g + 1))
                if not (isinstance(g, int) and g == 0):
                    dve.wait_ge(wlo_ready[O_], g)
                    dve.wait_ge(wsums_step, 2 * g)
                nc.vector.scalar_tensor_tensor(wg_sum[:], raw[O_][:], gm, wg_sum[:], ALU.mult, ALU.add)\
                    .then_inc(wsums_step, 1)
                nc.vector.scalar_tensor_tensor(wb_sum[:], raw[O_][:], bt, wb_sum[:], ALU.mult, ALU.add)\
                    .then_inc(wsums_step, 1)
                nc.vector.scalar_tensor_tensor(w_scaled[:], raw[O_][:], gm, gate_a[:], ALU.mult, ALU.mult)\
                    .then_inc(wscaled_ready, 1)

            dve.wait_ge(a_psum, KT * NS)
            scale_output_weights(0)

            def pick_pair(g):
                nc.vector.tensor_scalar(ncum_pair[:], ncum[:, :, bass.ds(2 * g, 2)], 1.0, None, ALU.mult)\
                    .then_inc(ncum_pair_ready, 1)

            dve.wait_ge(cols_ready, 2 * NS)
            pick_pair(0)

            def step(cur, nxt):
                if cur:
                    g, s = cur
                    u = NS * g + s
                    dve.wait_ge(btok_psum, u + 1)
                    wv = w_end[:, CH * s:CH * (s + 1), bass.ds(2 * g, 2)]
                    nc.vector.tensor_tensor(b_tok[:].rearrange("p c (a n) -> p c a n", a=2),
                                            ps[5][:].rearrange("p (c a n) -> p c a n", c=CH, a=2),
                                            wv.unsqueeze(3).to_broadcast([P, CH, 2, HD]), ALU.mult)\
                        .then_inc(btok_ready, 1)
                    dve.wait_ge(scores_psum, u + 1)
                    for a in range(2):
                        dve.wait_ge(decay_ready, 2 * u + a + 1)
                        nc.vector.tensor_tensor(dec[:, a, :], dec[:, a, :], ps[2 + a][:], ALU.mult)\
                            .then_inc(mixed_ready, 1)
                    if s == NS - 1 and not (isinstance(g, int) and g + 1 >= PAIRS):
                        pick_pair(g + 1)
                    dve.wait_ge(dstate_psum, u + 1)
                    dve.wait_ge(ecum_ready, u + 1)
                    for c in range(CH):
                        t = CH * s + c
                        wait(dve, state_step, 8 * u + 2 * c)
                        for a in range(2):
                            rows_a, cols_a = slice(HD * a, HD * (a + 1)), slice(HD * a, HD * (a + 1))
                            new = state[rows_a, (t + 1) % 8, cols_a]
                            if t + 1 == NT:
                                nc.vector.memset(new, 0.0).then_inc(state_step, 1)
                            else:
                                nc.vector.scalar_tensor_tensor(
                                    new, state[rows_a, t % 8, cols_a],
                                    e_cum[rows_a, (c + 1) * P - 1:(c + 1) * P],
                                    ps[4][rows_a, c * P + HD * a:c * P + HD * (a + 1)],
                                    ALU.mult, ALU.add).then_inc(state_step, 1)
                    dve.wait_ge(y_psum, u + 1)
                    dve.wait_ge(xT_ready, u + 1)
                    wait(dve, ylo_ready, u)
                    wait(dve, ystats_done, 2 * u)
                    nc.vector.scalar_tensor_tensor(y_raw[:], xT[:], skip_c[:, bass.ds(g, 1)], ps[5][:],
                                                   ALU.mult, ALU.add).then_inc(y_skip, 1)
                    dve.wait_ge(y_skip, u + 1)
                    dve.wait_ge(gate_ready, u + 1)
                    nc.vector.scalar_tensor_tensor(y_raw[:], y_raw[:], 0.5, gate[:], ALU.mult, ALU.mult)\
                        .then_inc(y_ready, 1)
                if nxt:
                    n = NS * nxt[0] + nxt[1]
                    dve.wait_ge(tanh_ready, n + 1)
                    nc.vector.scalar_tensor_tensor(gate[:], gate[:], 1.0, ps[1][:], ALU.add, ALU.mult)\
                        .then_inc(gate_ready, 1)
                if cur:
                    for c in range(CH):
                        dve.wait_ge(out_psum, CH * u + c + 1)
                        row = acc[:, CH * s + c, :]
                        if isinstance(g, int) and g == 0:
                            nc.vector.tensor_copy(row, ps[6 + c % 2][:]).then_inc(acc_added, 1)
                        else:
                            nc.vector.tensor_tensor(row, row, ps[6 + c % 2][:], ALU.add)\
                                .then_inc(acc_added, 1)
                    if s == NS - 1 and not (isinstance(g, int) and g + 1 >= PAIRS):
                        scale_output_weights(g + 1)
            mixer(dve, step)

            dve.wait_ge(wsums_step, 2 * PAIRS)
            link(nc.vector.tensor_tensor(wg_sum[:], wg_sum[:], gate_a[:], ALU.mult))
            link(nc.vector.tensor_tensor(wb_sum[:], wb_sum[:], gate_a[:], ALU.mult))
            nc.vector.engine_nop().then_inc(wsums_scaled, 1)
            dve.wait_ge(norm_psum, 1)
            nc.vector.tensor_copy(s1_row[:], ps[2][:]).then_inc(wsums_ready, 1)
            nc.vector.tensor_copy(beta_row[:], ps[3][:]).then_inc(wsums_ready, 1)
            dve.wait_ge(norm_psum, 2)
            link(nc.vector.tensor_copy(yst[:], ps[4][:, 0:4 * NT].rearrange("p (t n) -> p t n", n=4)))
            mean, meansq = yst[:, :, 0], yst[:, :, 2]
            link(nc.vector.tensor_tensor(yv[:, 1, :], mean, mean, ALU.mult))
            link(nc.vector.tensor_tensor(yv[:, 0, :], meansq, yv[:, 1, :], ALU.subtract))
            link(nc.vector.tensor_scalar(yst[:, :, 3], mean, -1.0, None, ALU.mult))
            nc.vector.tensor_scalar(yv[:, 0, :], yv[:, 0, :], EPS, None, ALU.add).then_inc(var_ready, 1)
            dve.wait_ge(var_ready, NS + 1)
            rsqrt(yv[:, 0, :], yv[:, 1, :], yv[:, 2, :], rs[:, 3, :], NS + 1)
            dve.wait_ge(wsums_ready, 2)
            for s in range(NS):
                for c in range(CH):
                    t = CH * s + c
                    link(nc.vector.scalar_tensor_tensor(acc[:, t, :], s1_row[:], yst[:, t, 3:4],
                                                        acc[:, t, :], ALU.mult, ALU.add))
                    dve.wait_ge(xb_ready, t + 1)
                    nc.vector.scalar_tensor_tensor(xin[:, c, :], acc[:, t, :], yv[:, 2, t:t + 1],
                                                   xin[:, c, :], ALU.mult, ALU.add).then_inc(x1_ready, 1)
                dve.wait_ge(x1_ready, CH * (s + 1))
                norm_rows(NS + s, NS + s + 2)
                modulate(NS + s, s, 8)

            def mlp_scale(g, j):
                dve.wait_ge(raw_loaded[2 + j], 16 * split_count(g, j))
                nc.vector.tensor_tensor(raw[2 + j][:], raw[2 + j][:], gate_b[:], ALU.mult)\
                    .then_inc(w2_scaled, 1)
                wait(dve, gelu_ready, NS * (g - 1) if isinstance(g, int) and g >= 2 or not isinstance(g, int) else 0)
                nc.vector.tensor_scalar(b1_pair[:, j:j + 1], b1_c[:, bass.ds(g, 1)], 1.0, None, ALU.mult)\
                    .then_inc(b1_ready, 1)
            for g in range(2):
                mlp_scale(g, g)
            dve.wait_ge(acc_set, NT)

            def mlp_step(cur, nxt):
                if cur:
                    g, s, j = cur
                    v = NS * g + s
                    for c in range(CH):
                        dve.wait_ge(mlp_psum, CH * v + c + 1)
                        row = acc[:, CH * s + c, :]
                        nc.vector.tensor_tensor(row, row, ps[2 + c][:], ALU.add).then_inc(mlp_added, 1)
                    if s == 1 and not (isinstance(g, int) and g + 2 >= HG):
                        mlp_scale(g + 2, j)
            mlp(dve, mlp_step)

        @block.tensor
        def _(pe):
            def three(bank, hi_l, lo_l, hi_r, lo_r, start, stop):
                nc.tensor.matmul(bank, lhsT=hi_l, rhs=hi_r, start=start, stop=False)
                nc.tensor.matmul(bank, lhsT=hi_l, rhs=lo_r, start=False, stop=False)
                return nc.tensor.matmul(bank, lhsT=lo_l, rhs=hi_r, start=False, stop=stop)

            pe.wait_ge(silu_ready, KT)
            for j in range(6):
                pe.wait_ge(wmod_loaded[j % 4], 16 * (j // 4 + 1))
                if j >= 2:
                    pe.wait_ge(mod_ready, j - 1)
                for k in range(KT):
                    ins = nc.tensor.matmul(ps[6 + j % 2][:], lhsT=silu_b[:, k, :], rhs=w_mod_sb[:, j % 4, k, :],
                                           start=k == 0, stop=k == KT - 1)
                ins.then_inc(mod_psum, 1)
            pe.wait_ge(consts_made, 8)
            pe.wait_ge(mod_ready, 6)
            for v in range(4):
                for k in range(KT):
                    at = 2 * (KT * v + k)
                    ins = nc.tensor.matmul(ps[1][:, at:at + 2], lhsT=mod_row[v][:, k * P:(k + 1) * P],
                                           rhs=pick0[:], start=True, stop=True)
            ins.then_inc(modcol_psum, 1)

            def transpose_rows(i):
                pe.wait_ge(xn_ready, CH * (i + 1))
                for k in range(KT):
                    wait(pe, hraw_ready, KT * (i - 1) + k + 1)
                    for c in range(CH):
                        ins = nc.tensor.transpose(ps[2 + k][:, c * P:(c + 1) * P],
                                                  xin[:, c, k * P:(k + 1) * P], ident[:])
                    ins.then_inc(xnT_psum, 1)

            pe.wait_ge(const_loaded, 16 * 6)
            pe.wait_ge(modcol_ready, 2)
            for s in range(NS):
                transpose_rows(s)
                wait(pe, ea_ready, s)
                for k in range(KT):
                    pe.wait_ge(hraw_ready, KT * s + k + 1)
                    ins = nc.tensor.matmul(ps[0][0:HEADS, :], lhsT=wa[:, k, :], rhs=h_raw[k % 2][:],
                                           start=k == 0, stop=k == KT - 1)
                    ins.then_inc(a_psum, 1)
                wait(pe, cols_ready, 2 * s)
                pe.wait_ge(cum_ready, CH * (s + 1))
                pe.wait_ge(wend_ready, s + 1)
                for j, src in enumerate((cum_r, wend_r)):
                    for c in range(CH):
                        at = j * P + c * HEADS
                        ins = nc.tensor.transpose(ps[1][:, at:at + HEADS], src[:, c * P:(c + 1) * P],
                                                  ident[0:HEADS, 0:HEADS])
                ins.then_inc(cols_psum, 1)

            pe.wait_ge(cols_ready, 2 * NS)
            pe.wait_ge(hlo_ready, KT * NS)
            pe.wait_ge(hhi_ready, KT * NS)

            def project(m, g, s, bank, done):
                if s == 0:
                    pe.wait_ge(whi_ready[m], g + 1)
                    pe.wait_ge(wlo_ready[m], g + 1)
                tokens = slice(s * SUP, (s + 1) * SUP)
                for k in range(KT):
                    cols = slice(k * P, (k + 1) * P)
                    ins = three(ps[bank][:], w_hi[m][:, cols], w_lo[m][:, cols], hT_hi[:, k, tokens],
                                hT_lo[:, k, tokens], k == 0, k == KT - 1)
                ins.then_inc(done, 1)

            def step(cur, nxt):
                if cur:
                    g, s = cur
                    u = NS * g + s
                    pe.wait_ge(xT_ready, u + 1)
                    pe.wait_ge(ecum_ready, u + 1)
                    for c in range(CH):
                        part = slice(c * P, (c + 1) * P)
                        ins = nc.tensor.transpose(ps[4][:, part], xT[:, part], ident[:])
                    ins.then_inc(xtok_psum, 1)
                    pe.wait_ge(bT_ready, u + 1)
                    wait(pe, y_skip, u)
                    for c in range(CH):
                        part = slice(c * P, (c + 1) * P)
                        ins = nc.tensor.transpose(ps[5][:, part], bT[:, part], ident[:])
                    ins.then_inc(btok_psum, 1)
                    pe.wait_ge(cT_ready, u + 1)
                    pe.wait_ge(decay_ready, 2 * (u + 1))
                    for c in range(CH):
                        part = slice(c * P, (c + 1) * P)
                        for a in range(2):
                            head = slice(HD * a, HD * (a + 1))
                            ins = nc.tensor.matmul(ps[2 + a][:, part], lhsT=bT[head, part], rhs=cT[head, part],
                                                   start=True, stop=True)
                    ins.then_inc(scores_psum, 1)
                if nxt:
                    gn, sn = nxt
                    n = NS * gn + sn
                    wait(pe, xT_ready, n)
                    project(B_, gn, sn, 0, bT_psum)
                if cur:
                    pe.wait_ge(xtok_ready, u + 1)
                    pe.wait_ge(btok_ready, u + 1)
                    for c in range(CH):
                        ins = nc.tensor.matmul(ps[4][:, c * P:(c + 1) * P], lhsT=b_tok[:, c, :],
                                               rhs=x_tok[:, c, :], start=True, stop=True)
                    ins.then_inc(dstate_psum, 1)
                if nxt:
                    wait(pe, gate_ready, n)
                    project(C_, gn, sn, 1, cT_psum)
                if cur:
                    pe.wait_ge(state_step, 8 * (u + 1))
                    pe.wait_ge(cdec_ready, u + 1)
                    for c in range(CH):
                        part = slice(c * P, (c + 1) * P)
                        nc.tensor.matmul(ps[5][:, part], lhsT=state[:, (CH * s + c) % 8, :], rhs=c_dec[:, part],
                                         start=c == 0, stop=False, skip_group_check=True)
                    pe.wait_ge(mixed_ready, 2 * (u + 1))
                    for c in range(CH):
                        part = slice(c * P, (c + 1) * P)
                        for a in range(2):
                            head = slice(HD * a, HD * (a + 1))
                            ins = nc.tensor.matmul(ps[5][head, part], lhsT=x_tok[:, c, head],
                                                   rhs=dec[:, a, part], start=False, stop=True,
                                                   skip_group_check=True)
                    ins.then_inc(y_psum, 1)
                if nxt:
                    pe.wait_ge(bT_ready, n + 1)
                    project(X_, gn, sn, 0, xT_psum)
                    pe.wait_ge(rows_loaded[sn % 2], 16 * (2 * gn + sn // 2 + 1))
                    wait(pe, mixed_ready, 2 * n)
                    wait(pe, state_step, 8 * n)
                    for a in range(2):
                        nc.tensor.matmul(ps[2 + a][:], lhsT=sel[:, a, :], rhs=rows[sn % 2][:], start=True,
                                         stop=False)
                        nc.tensor.matmul(ps[2 + a][:], lhsT=ident_b[:],
                                         rhs=causal[:].unsqueeze(1).to_broadcast([P, CH, P]), start=False,
                                         stop=True).then_inc(decay_psum, 1)
                    nc.tensor.matmul(ps[4][:], lhsT=sel[:, 2, :], rhs=rows[sn % 2][:], start=True, stop=True)\
                        .then_inc(decay_psum, 1)
                    pe.wait_ge(cT_ready, n + 1)
                    project(Z_, gn, sn, 1, zT_psum)
                if cur:
                    pe.wait_ge(yhi_ready, u + 1)
                    pe.wait_ge(ylo_ready, u + 1)
                    if s == 0:
                        pe.wait_ge(whi_ready[O_], g + 1)
                        pe.wait_ge(wlo_ready[O_], g + 1)
                    for c in range(CH):
                        part = slice(c * P, (c + 1) * P)
                        wait(pe, acc_added, CH * u + c - 1)
                        three(ps[6 + c % 2][:], y_hi[:, 0, part], y_lo[:, 0, part], w_hi[O_][:], w_lo[O_][:],
                              True, True).then_inc(out_psum, 1)
            mixer(pe, step)

            pe.wait_ge(wsums_scaled, 1)
            nc.tensor.matmul(ps[2][:], lhsT=ones[:], rhs=wg_sum[:], start=True, stop=True)
            nc.tensor.matmul(ps[3][:], lhsT=ones[:], rhs=wb_sum[:], start=True, stop=True)\
                .then_inc(norm_psum, 1)
            pe.wait_ge(ystats_done, 2 * NS * PAIRS)
            for t in range(NT):
                part = slice(t * P, (t + 1) * P)
                nc.tensor.matmul(ps[4][:, 4 * t:4 * t + 2], lhsT=y_sum[:, part], rhs=mean_w[:], start=True,
                                 stop=True)
                ins = nc.tensor.matmul(ps[4][:, 4 * t + 2:4 * t + 4], lhsT=yy_sum[:, part], rhs=mean_w[:],
                                       start=True, stop=True)
            ins.then_inc(norm_psum, 1)
            pe.wait_ge(var_ready, NS + 1)
            pe.wait_ge(wsums_ready, 2)
            for s in range(NS):
                transpose_rows(NS + s)
            pe.wait_ge(hlo_ready, 2 * KT * NS)
            pe.wait_ge(hhi_ready, 2 * KT * NS)

            def mlp_step(cur, nxt):
                if nxt:
                    g, s, j = nxt
                    v = NS * g + s
                    if s == 0:
                        pe.wait_ge(whi_ready[j], split_count(g, j))
                        pe.wait_ge(wlo_ready[j], split_count(g, j))
                    wait(pe, gelu_ready, v - 1)
                    tokens = slice(s * SUP, (s + 1) * SUP)
                    for k in range(KT):
                        cols = slice(k * P, (k + 1) * P)
                        ins = three(ps[s % 2][:], w_hi[j][:, cols], w_lo[j][:, cols], hT_hi[:, k, tokens],
                                    hT_lo[:, k, tokens], k == 0, k == KT - 1)
                    ins.then_inc(hid_psum, 1)
                if cur:
                    g, s, j = cur
                    v = NS * g + s
                    if s == 0:
                        pe.wait_ge(whi_ready[2 + j], split_count(g, j))
                        pe.wait_ge(wlo_ready[2 + j], split_count(g, j))
                    pe.wait_ge(ghi_ready, v + 1)
                    pe.wait_ge(glo_ready, v + 1)
                    for c in range(CH):
                        part = slice(c * P, (c + 1) * P)
                        wait(pe, mlp_added, CH * (v - 1) + c + 1)
                        three(ps[2 + c][:], y_hi[:, s % 2, part], y_lo[:, s % 2, part], w_hi[2 + j][:],
                              w_lo[2 + j][:], True, True).then_inc(mlp_psum, 1)
            mlp(pe, mlp_step)


_OUT = "out_dram"


def kernel(**inputs):
    import numpy as _np
    import concourse.bacc as _bacc
    from concourse import mybir as _mybir
    from concourse.bass_utils import run_bass_kernel_spmd as _run

    def rows(name, *shape):
        return _np.asarray(inputs[name]).reshape(shape)

    def cols(name):
        return rows(name, -1, P).T

    def ktiles(w, n):
        return w.reshape(-1, n, KT, P).transpose(0, 3, 2, 1)

    w_in = _np.asarray(inputs["L0_attn_W_in"])
    main = ktiles(w_in[:4 * INNER], P).reshape(4, PAIRS, P, KT * P)[[2, 3, 0, 1]].transpose(1, 0, 2, 3)
    laid = {
        "x": rows("L0_attn_x", TOKENS, E),
        "w_pairs": main,
        "w_decay": ktiles(w_in[4 * INNER:], HEADS)[0],
        "w_out": _np.asarray(inputs["L0_attn_W_out"]).T.reshape(PAIRS, P, E),
        "gamma": cols("L0_attn_gamma"),
        "beta": cols("L0_attn_beta"),
        "skip": cols("L0_attn_D"),
        "w1": ktiles(_np.asarray(inputs["L0_ffn_proj1"]), P).reshape(HG, P, KT * P),
        "b1": cols("L0_ffn_proj1_bias"),
        "w2": _np.asarray(inputs["L0_ffn_proj2"]).T.reshape(HG, P, E),
        "b2": rows("L0_ffn_proj2_bias", E),
        "cond": cols("L0_c"),
        "w_mod": rows("L0_wmod", KT, P, 6, E).transpose(2, 1, 0, 3),
    }
    nc = _bacc.Bacc("TRN2", target_bir_lowering=False, num_devices=1)
    arrays, args = {}, {}
    for name, a in laid.items():
        a = _np.ascontiguousarray(a)
        arrays[f"{name}_dram"] = a
        args[name] = nc.dram_tensor(f"{name}_dram", a.shape, _mybir.dt.from_np(a.dtype), kind="ExternalInput").ap()
    args["out"] = nc.dram_tensor(_OUT, (TOKENS, E), F32, kind="ExternalOutput").ap()
    adaln_block(nc, **args)
    r = _run(nc, [arrays], core_ids=[0])
    return r.results[0][_OUT].reshape(1, TOKENS, E)
```

```python
from contextlib import ExitStack

import concourse.bass as bass
from concourse import mybir

ALU = mybir.AluOpType
ACT = mybir.ActivationFunctionType
F32 = mybir.dt.float32
F32R = mybir.dt.float32r
BF16 = mybir.dt.bfloat16

P = 128
TOKENS = 2048
E = 512
KT = E // P
HEADS = 32
HD = 64
INNER = HEADS * HD
PAIRS = INNER // P
SUP = 512
CH = SUP // P
NS = TOKENS // SUP
NT = TOKENS // P
HID = 2048
HG = HID // P
EPS = 1e-5
NEG = -1e30
B_, C_, X_, Z_, O_ = range(5)


def adaln_block(nc, x, w_pairs, w_decay, w_out, gamma, beta, skip, w1, b1, w2, b2, cond, w_mod, out):
    crows = nc.dram_tensor("cum_rows_scratch", (HEADS, 3, TOKENS), BF16, kind="Internal").ap()

    with ExitStack() as ctx:
        def sb(name, shape, dt=F32):
            return ctx.enter_context(nc.sbuf_tensor(name, shape, dt))

        def sem(name):
            return ctx.enter_context(nc.semaphore(name))

        ps = [ctx.enter_context(nc.psum_tensor(f"bank{i}", [P, 512], F32)) for i in range(8)]

        hT_hi = sb("hT_hi", [P, KT, TOKENS], F32R)
        hT_lo = sb("hT_lo", [P, KT, TOKENS], F32R)
        acc = sb("acc", [P, NT, E])
        y_sum = sb("y_sum", [P, TOKENS])
        yy_sum = sb("yy_sum", [P, TOKENS])
        raws = sb("raws", [P, 5, 512])
        raw = [raws[:, m, :] for m in range(5)]
        w_hi = [sb(f"w_hi{m}", [P, 512], F32R) for m in range(5)]
        w_lo = [sb(f"w_lo{m}", [P, 512], F32R) for m in range(5)]
        w_scaled = sb("w_scaled", [P, E])
        wg_sum = sb("wg_sum", [P, E])
        wb_sum = sb("wb_sum", [P, E])
        bT = sb("bT", [P, SUP])
        cT = sb("cT", [P, SUP])
        xT = sb("xT", [P, SUP])
        gate = sb("gate", [P, SUP])
        x_tok = sb("x_tok", [P, CH, P])
        b_tok = sb("b_tok", [P, CH, P])
        dec = sb("dec", [P, 2, SUP])
        e_cum = sb("e_cum", [P, SUP])
        c_dec = sb("c_dec", [P, SUP])
        state = sb("state", [P, 8, P])
        y_raw = sb("y_raw", [P, SUP])
        y_sq = sb("y_sq", [P, SUP])
        y_hi = sb("y_hi", [P, 2, SUP], F32R)
        y_lo = sb("y_lo", [P, 2, SUP], F32R)
        rows = [sb(f"rows{i}", [6, SUP], BF16) for i in range(2)]
        xin = sb("xin", [P, CH, E])
        gate_a = sb("gate_a", [P, E])
        gate_b = sb("gate_b", [P, E])
        gb_b2 = sb("gb_b2", [P, E])
        ncum = sb("ncum", [P, NT, HEADS])
        w_end = sb("w_end", [P, NT, HEADS])
        ncum_pair = sb("ncum_pair", [P, NT, 2])
        b1_pair = sb("b1_pair", [P, 2])
        ident = sb("ident", [P, P])
        ident_b = sb("ident_b", [P, P], BF16)
        causal = sb("causal", [P, P], BF16)
        sel = sb("sel", [6, 3, P], BF16)
        ones = sb("ones", [P, P])
        pick0 = sb("pick0", [P, 2])
        mean_w = sb("mean_w", [P, 2])
        mod_col = sb("mod_col", [P, 16, 2])
        gamma_c = sb("gamma_c", [P, PAIRS])
        beta_c = sb("beta_c", [P, PAIRS])
        skip_c = sb("skip_c", [P, PAIRS])
        b1_c = sb("b1_c", [P, HG])
        cc = sb("cc", [P, 4, KT])
        bst = sb("bst", [P, CH, 6])
        mv = sb("mv", [P, CH, 2])
        rs = sb("rs", [P, 4, NT])
        yst = sb("yst", [P, NT, 4])
        yv = sb("yv", [P, 3, NT])
        w_mod_sb = acc[:, 0:8, :].rearrange("p (j k) e -> p j k e", j=2)
        h_raw1 = [acc[:, 8 + k, :] for k in range(KT)]
        ea = acc[0:HEADS, 12, :]
        cum_r = acc[0:HEADS, 13, :]
        rest = acc[0:HEADS, 8, :]
        parts = acc[0:HEADS, 14:16, :].rearrange("p a n -> p (a n)").bitcast(BF16)[:, 0:3 * SUP]\
            .rearrange("p (j n) -> p j n", j=3)
        w_dec = acc[:, 15, 384:512].rearrange("p (k h) -> p k h", k=KT)
        silu_b = dec[:, 0, :].rearrange("p (k m) -> p k m", k=KT)
        mod_row = [bT, cT, xT, x_tok[:, :, :].rearrange("p c m -> p (c m)")]
        b2_row = gate
        gelu = [y_raw, y_sq]
        h_raw2 = [raw[O_], w_scaled]
        s1_row, beta_row = wg_sum, wb_sum

        def h_raw(i, k):
            return h_raw1[k] if i < NS else h_raw2[k % 2]

        def x_buf(i):
            return raws[:, 0:CH, :] if i == NS else xin

        const_loaded = sem("const_loaded")
        cond_loaded = sem("cond_loaded")
        wmod_loaded = [sem(f"wmod_loaded{i}") for i in range(2)]
        x_loaded = [sem(f"x_loaded{i}") for i in range(2)]
        raw_loaded = [sem(f"raw_loaded{m}") for m in range(5)]
        rows_loaded = [sem(f"rows_loaded{i}") for i in range(2)]
        crows_stored = sem("crows_stored")
        out_stored = sem("out_stored")
        consts_made = sem("consts_made")
        silu_exp = sem("silu_exp")
        silu_ready = sem("silu_ready")
        mod_psum = sem("mod_psum")
        mod_ready = sem("mod_ready")
        modcol_psum = sem("modcol_psum")
        modcol_ready = sem("modcol_ready")
        dve_chain = sem("dve_chain")
        zeroed = sem("zeroed")
        var_ready = sem("var_ready")
        std_ready = sem("std_ready")
        xn_ready = sem("xn_ready")
        xnT_psum = sem("xnT_psum")
        hraw_ready = sem("hraw_ready")
        hhi_ready = sem("hhi_ready")
        hlo_ready = sem("hlo_ready")
        ea_ready = sem("ea_ready")
        cum_ready = sem("cum_ready")
        wend_arg = sem("wend_arg")
        wend_ready = sem("wend_ready")
        parts_ready = sem("parts_ready")
        cols_psum = sem("cols_psum")
        cols_ready = sem("cols_ready")
        whi_ready = [sem(f"whi_ready{m}") for m in range(5)]
        wlo_ready = [sem(f"wlo_ready{m}") for m in range(5)]
        wscaled_ready = sem("wscaled_ready")
        bT_psum, cT_psum, xT_psum, zT_psum = (sem(f"{n}T_psum") for n in "bcxz")
        bT_ready, cT_ready, xT_ready, tanh_ready = (sem(f"{n}_ready") for n in ("bT", "cT", "xT", "tanh"))
        gate_ready = sem("gate_ready")
        xtok_psum, btok_psum = sem("xtok_psum"), sem("btok_psum")
        xtok_ready, btok_ready = sem("xtok_ready"), sem("btok_ready")
        scores_psum = sem("scores_psum")
        decay_psum = sem("decay_psum")
        decay_ready = sem("decay_ready")
        ecum_ready = sem("ecum_ready")
        cdec_ready = sem("cdec_ready")
        mixed_ready = sem("mixed_ready")
        dstate_psum = sem("dstate_psum")
        state_step = sem("state_step")
        y_psum = sem("y_psum")
        y_skip = sem("y_skip")
        y_ready = sem("y_ready")
        yhi_ready = sem("yhi_ready")
        ylo_ready = sem("ylo_ready")
        ystats_done = sem("ystats_done")
        out_psum = sem("out_psum")
        acc_added = sem("acc_added")
        wsums_ready = sem("wsums_ready")
        xb_ready = sem("xb_ready")
        x1_ready = sem("x1_ready")
        acc_set = sem("acc_set")
        w2_scaled = sem("w2_scaled")
        hid_psum = sem("hid_psum")
        gelu_ready = sem("gelu_ready")
        ghi_ready = sem("ghi_ready")
        glo_ready = sem("glo_ready")
        mlp_psum = sem("mlp_psum")
        mlp_added = sem("mlp_added")
        wsums_step = sem("wsums_step")
        ncum_pair_ready = sem("ncum_pair_ready")
        b1_ready = sem("b1_ready")
        wsums_scaled = sem("wsums_scaled")
        wsums_psum = sem("wsums_psum")
        ystat_psum = sem("ystat_psum")
        ystat_read = sem("ystat_read")
        yvar_ready = sem("yvar_ready")
        ystd_ready = sem("ystd_ready")
        ysq_ready = sem("ysq_ready")
        a_psum = sem("a_psum")

        def wait(eng, s, value):
            if not (isinstance(value, int) and value <= 0):
                eng.wait_ge(s, value)

        def after(g, s):
            return (g, s + 1) if s + 1 < NS else (g + 1, 0)

        def mixer(eng, step):
            step(None, (0, 0))
            for s in range(NS):
                step((0, s), after(0, s))
            with eng.Fori(1, PAIRS - 1) as g:
                for s in range(NS):
                    step((g, s), after(g, s))
            for s in range(NS):
                step((PAIRS - 1, s), after(PAIRS - 1, s) if s + 1 < NS else None)

        def mlp(eng, step, tail):
            def pair(g0, last, done=0):
                for j in range(2):
                    for s in range(NS):
                        if NS * j + s < done:
                            continue
                        end = last and j == 1 and s + 1 == NS
                        nxt = (g0 + j, s + 1, j) if s + 1 < NS else (g0 + j + 1, 0, 1 - j)
                        step((g0 + j, s, j), None if end else nxt)
            step(None, (0, 0, 0))
            tail(NS + 2)
            step((0, 0, 0), (0, 1, 0))
            tail(NS + 3)
            pair(0, False, 1)
            with eng.Fori(1, HG // 2 - 1) as r:
                pair(r * 2, False)
            pair(HG - 2, True)

        def first_pair(nxt):
            return nxt is not None and isinstance(nxt[0], int) and nxt[0] == 0

        def last_pair(cur):
            return cur is not None and isinstance(cur[0], int) and cur[0] == PAIRS - 1

        def norm_at(cur, nxt):
            if first_pair(nxt) and nxt[1] + 1 < NS:
                return nxt[1] + 1
            if last_pair(cur) and cur[1] >= 2:
                return NS + cur[1] - 2
            return None

        def stats_at(cur, nxt):
            if first_pair(nxt) and nxt[1] + 2 < NS:
                return nxt[1] + 2
            if last_pair(cur) and cur[1] >= 1:
                return NS + cur[1] - 1
            return None

        def wait_x(eng, i):
            if i == NS:
                eng.wait_ge(x_loaded[1], 16)
            else:
                eng.wait_ge(x_loaded[0], 16 * (i + 1 if i < NS else i))

        def split_count(g, j):
            return PAIRS + (g - j) // 2 + 1

        x_rows = x.rearrange("(s c p) e -> s p c e", p=P, c=CH)
        out_rows = out.rearrange("(s c p) e -> s p c e", p=P, c=CH)

        block = ctx.enter_context(nc.Block())

        @block.sync
        def _(sp):
            sp.dma_start(cc[:, 0, :], cond).then_inc(cond_loaded, 16)
            for j in range(2):
                sp.dma_start(w_mod_sb[:, j], w_mod[j]).then_inc(wmod_loaded[j], 16)
            sp.dma_start(xin[:], x_rows[0]).then_inc(x_loaded[0], 16)
            sp.dma_start(w_dec[:], w_decay).then_inc(const_loaded, 16)
            for m in (B_, C_):
                sp.dma_start(raw[m], w_pairs[0, m]).then_inc(raw_loaded[m], 16)
            for dst, src in ((gamma_c, gamma), (beta_c, beta), (skip_c, skip), (b1_c, b1)):
                sp.dma_start(dst[:], src).then_inc(const_loaded, 16)
            sp.dma_start(b2_row[:], b2.partition_broadcast(P)).then_inc(const_loaded, 16)
            sp.wait_ge(mod_psum, 1)
            sp.dma_start(w_mod_sb[:, 0], w_mod[2]).then_inc(wmod_loaded[0], 16)
            for m in (X_, Z_):
                sp.dma_start(raw[m], w_pairs[0, m]).then_inc(raw_loaded[m], 16)
            sp.dma_start(raw[O_], w_out[0]).then_inc(raw_loaded[O_], 16)
            sp.wait_ge(xnT_psum, KT)
            sp.dma_start(xin[:], x_rows[1]).then_inc(x_loaded[0], 16)
            for j in range(3, 6):
                sp.wait_ge(mod_psum, j - 1)
                sp.dma_start(w_mod_sb[:, j % 2], w_mod[j]).then_inc(wmod_loaded[j % 2], 16)

            def store_rows(i):
                sp.wait_ge(parts_ready, i + 1)
                sp.dma_start(crows[:, :, i * SUP:(i + 1) * SUP], parts).then_inc(crows_stored, 16)

            store_rows(0)

            def step(cur, nxt):
                if nxt:
                    g, s = nxt
                    if first_pair(nxt):
                        sp.wait_ge(crows_stored, 16 * (s + 1))
                    wait(sp, decay_psum, 3 * (NS * g + s - 1))
                    src = crows[bass.ds(2 * g, 2), :, s * SUP:(s + 1) * SUP].rearrange("a j n -> (a j) n")
                    sp.dma_start(rows[s % 2][:], src).then_inc(rows_loaded[s % 2], 16)
                if cur and cur[1] == 0 and not (isinstance(cur[0], int) and cur[0] + 1 >= PAIRS):
                    g = cur[0] + 1
                    for m in range(5):
                        sp.wait_ge(wlo_ready[m] if m < O_ else wscaled_ready, g)
                        src = w_pairs[bass.ds(g, 1), m] if m < O_ else w_out[bass.ds(g, 1)]
                        sp.dma_start(raw[m], src.rearrange("a p n -> (a p) n"))\
                            .then_inc(raw_loaded[m], 16)
                if last_pair(cur) and cur[1] == 0:
                    for m in range(4):
                        sp.wait_ge(wlo_ready[m], PAIRS)
                    for i in (NS, NS + 1):
                        sp.dma_start(x_buf(i)[:, :, :], x_rows[i - NS]).then_inc(x_loaded[i == NS], 16)
                i = norm_at(cur, nxt)
                if i is not None and i not in (NS - 1, NS):
                    sp.wait_ge(xnT_psum, KT * (i + 1))
                    sp.dma_start(xin[:], x_rows[(i + 1) % NS]).then_inc(x_loaded[0], 16)
                if i == NS:
                    sp.wait_ge(xnT_psum, KT * (i + 1))
                    for g in range(2):
                        sp.dma_start(raw[g], w1[g]).then_inc(raw_loaded[g], 16)
                        sp.dma_start(raw[2 + g], w2[g]).then_inc(raw_loaded[2 + g], 16)
                if first_pair(nxt) and nxt[1] + 1 < NS:
                    store_rows(nxt[1] + 1)
            mixer(sp, step)

            def tail(i):
                if i == NS + 2:
                    sp.wait_ge(xnT_psum, KT * (i + 1))
                    sp.dma_start(xin[:], x_rows[3]).then_inc(x_loaded[0], 16)

            def mlp_step(cur, nxt):
                if cur and cur[1] == 0 and not (isinstance(cur[0], int) and cur[0] + 2 >= HG):
                    g, _, j = cur
                    for m, src in ((j, w1), (2 + j, w2)):
                        sp.wait_ge(wlo_ready[m], split_count(g, j))
                        sp.dma_start(raw[m], src[bass.ds(g + 2, 1)].rearrange("a p n -> (a p) n"))\
                            .then_inc(raw_loaded[m], 16)
                if cur and isinstance(cur[0], int) and cur[0] == HG - 1:
                    s = cur[1]
                    sp.wait_ge(mlp_added, CH * (NS * cur[0] + s + 1))
                    sp.dma_start(out_rows[s], acc[:, CH * s:CH * (s + 1), :]).then_inc(out_stored, 16)
            mlp(sp, mlp_step, tail)
            sp.wait_ge(out_stored, 16 * NS)

        @block.gpsimd
        def _(pool):
            for t, value in ((ones, 1.0), (ident, 0.0), (ident_b, 0.0), (causal, 0.0), (sel, 1.0),
                             (pick0, 0.0), (mean_w, 1.0 / INNER)):
                nc.gpsimd.memset(t[:], value).then_inc(consts_made, 1)
            pool.wait_ge(consts_made, 7)
            for m in (ident, ident_b):
                nc.gpsimd.affine_select(out=m[:], in_=m[:], compare_op=ALU.not_equal, fill=1.0, base=0,
                                        pattern=[[-1, P]], channel_multiplier=1).then_inc(consts_made, 1)
            nc.gpsimd.affine_select(out=causal[:], in_=causal[:], compare_op=ALU.is_ge, fill=NEG, base=0,
                                    pattern=[[1, P]], channel_multiplier=-1).then_inc(consts_made, 1)
            first = dict(compare_op=ALU.is_ge, fill=0.0, base=2, channel_multiplier=-1)
            second = dict(compare_op=ALU.is_ge, fill=0.0, base=-3, channel_multiplier=1)
            for view, n, which in ((sel[:, 0, :], P, first), (sel[:, 1, :], P, second),
                                   (sel[:, 2, 0:HD], HD, first), (sel[:, 2, HD:P], HD, second)):
                nc.gpsimd.affine_select(out=view, in_=view, pattern=[[0, n]], **which)\
                    .then_inc(consts_made, 1)
            nc.gpsimd.memset(pick0[0:1, :], 1.0).then_inc(consts_made, 1)
            for t in (wg_sum, wb_sum, y_sum, yy_sum, state):
                nc.gpsimd.memset(t[:], 0.0).then_inc(zeroed, 1)

            def hT_low(i, k):
                tokens = slice(i % NS * SUP, (i % NS + 1) * SUP)
                pool.wait_ge(hraw_ready, KT * i + k + 1)
                pool.wait_ge(hhi_ready, KT * i + k + 1)
                nc.gpsimd.tensor_tensor(hT_lo[:, k, tokens], h_raw(i, k)[:, :], hT_hi[:, k, tokens].bitcast(F32),
                                        ALU.subtract).then_inc(hlo_ready, 1)

            def split_low(m, source, count):
                pool.wait_ge(whi_ready[m], count)
                nc.gpsimd.tensor_tensor(w_lo[m][:], source[:, :], w_hi[m][:].bitcast(F32), ALU.subtract)\
                    .then_inc(wlo_ready[m], 1)

            for k in range(KT):
                hT_low(0, k)
            for m in range(5):
                split_low(m, raw[m] if m < O_ else w_scaled, 1)

            def add_beta_row(i):
                wait_x(pool, i)
                pool.wait_ge(wsums_ready, 2)
                for c in range(CH):
                    row = x_buf(i)[:, c, :]
                    nc.gpsimd.tensor_tensor(row, row, beta_row[:], ALU.add).then_inc(xb_ready, 1)

            def set_acc(i):
                for c in range(CH):
                    t = CH * (i - NS) + c
                    pool.wait_ge(x1_ready, t + 1)
                    nc.gpsimd.tensor_tensor(acc[:, t, :], x_buf(i)[:, c, :], gb_b2[:], ALU.add)\
                        .then_inc(acc_set, 1)

            def step(cur, nxt):
                more = nxt and nxt[1] == NS - 1 and not (isinstance(nxt[0], int) and nxt[0] + 1 >= PAIRS)
                i = norm_at(cur, nxt)
                if cur:
                    g, s = cur
                    u = NS * g + s
                    pool.wait_ge(ecum_ready, u + 1)
                    pool.wait_ge(cT_ready, u + 1)
                    nc.gpsimd.tensor_tensor(c_dec[:], cT[:], e_cum[:], ALU.mult).then_inc(cdec_ready, 1)
                    if s == 0 and not (isinstance(g, int) and g == 0):
                        split_low(O_, w_scaled, g + 1)
                if more:
                    split_low(B_, raw[B_], nxt[0] + 2)
                    split_low(C_, raw[C_], nxt[0] + 2)
                if i is not None:
                    hT_low(i, 0)
                    hT_low(i, 1)
                if cur:
                    tokens = slice(s * SUP, (s + 1) * SUP)
                    pool.wait_ge(y_ready, u + 1)
                    pool.wait_ge(yhi_ready, u + 1)
                    nc.gpsimd.tensor_tensor(y_lo[:, 0, :], y_raw[:], y_hi[:, 0, :].bitcast(F32),
                                            ALU.subtract).then_inc(ylo_ready, 1)
                    wait(pool, ystats_done, 2 * u)
                    nc.gpsimd.tensor_tensor(y_sum[:, tokens], y_sum[:, tokens], y_raw[:], ALU.add)\
                        .then_inc(ystats_done, 1)
                    pool.wait_ge(ysq_ready, u + 1)
                    nc.gpsimd.tensor_tensor(yy_sum[:, tokens], yy_sum[:, tokens], y_sq[:], ALU.add)\
                        .then_inc(ystats_done, 1)
                if i is not None:
                    hT_low(i, 2)
                    hT_low(i, 3)
                if more:
                    split_low(X_, raw[X_], nxt[0] + 2)
                    split_low(Z_, raw[Z_], nxt[0] + 2)
                if last_pair(cur) and s >= 1:
                    add_beta_row(NS + s - 1)
                    set_acc(NS + s - 1)
            mixer(pool, step)

            def mlp_split(g, j):
                count = split_count(g, j)
                split_low(j, raw[j], count)
                split_low(2 + j, raw[2 + j], count)
            for g in range(2):
                mlp_split(g, g)

            def tail(i):
                for k in range(KT):
                    hT_low(i, k)
                if i == NS + 2:
                    add_beta_row(NS + 3)
                    set_acc(NS + 3)

            def mlp_step(cur, nxt):
                if nxt:
                    g, s, j = nxt
                    v = NS * g + s
                    pool.wait_ge(gelu_ready, v + 1)
                    pool.wait_ge(ghi_ready, v + 1)
                    nc.gpsimd.tensor_tensor(y_lo[:, s % 2, :], gelu[s % 2][:], y_hi[:, s % 2, :].bitcast(F32),
                                            ALU.subtract).then_inc(glo_ready, 1)
                if cur and cur[1] == NS - 1 and not (isinstance(cur[0], int) and cur[0] + 2 >= HG):
                    mlp_split(cur[0] + 2, cur[2])
            mlp(pool, mlp_step, tail)

        @block.scalar
        def _(act):
            act.wait_ge(cond_loaded, 16)
            nc.scalar.activation(cc[:, 1, :], cc[:, 0, :], ACT.Exp, scale=-1.0).then_inc(silu_exp, 1)

            def hT_high(i, k):
                tokens = slice(i % NS * SUP, (i % NS + 1) * SUP)
                act.wait_ge(hraw_ready, KT * i + k + 1)
                nc.scalar.copy(hT_hi[:, k, tokens], h_raw(i, k)[:, :]).then_inc(hhi_ready, 1)

            def row_std(i):
                act.wait_ge(var_ready, i + 1)
                nc.scalar.activation(rs[:, 1, 0:CH], rs[:, 0, 0:CH], ACT.Sqrt).then_inc(std_ready, 1)

            def mixer_std(s):
                act.wait_ge(yvar_ready, s + 1)
                part = slice(CH * s, CH * (s + 1))
                nc.scalar.activation(yv[:, 1, part], yv[:, 0, part], ACT.Sqrt).then_inc(ystd_ready, 1)

            def exp_a(i):
                act.wait_ge(a_psum, i + 1)
                nc.scalar.activation(ea, ps[6][0:HEADS, :], ACT.Exp).then_inc(ea_ready, 1)

            def decay_to_end(i):
                act.wait_ge(wend_arg, i + 1)
                nc.scalar.activation(ea, ea, ACT.Exp, scale=-1.0).then_inc(wend_ready, 1)

            row_std(0)
            for k in range(KT):
                hT_high(0, k)
            exp_a(0)
            decay_to_end(0)

            def split_high(m, source):
                nc.scalar.copy(w_hi[m][:], source[:, :]).then_inc(whi_ready[m], 1)

            for m in range(4):
                act.wait_ge(raw_loaded[m], 16)
                split_high(m, raw[m])
            act.wait_ge(wscaled_ready, 1)
            split_high(O_, w_scaled)

            def step(cur, nxt):
                more = nxt and nxt[1] == NS - 1 and not (isinstance(nxt[0], int) and nxt[0] + 1 >= PAIRS)

                def next_weights(m):
                    if more:
                        act.wait_ge(raw_loaded[m], 16 * (nxt[0] + 2))
                        split_high(m, raw[m])

                i = norm_at(cur, nxt)
                if cur:
                    g, s = cur
                    u = NS * g + s
                    act.wait_ge(xtok_psum, u + 1)
                    nc.scalar.copy(x_tok[:].rearrange("p c m -> p (c m)"), ps[4][:]).then_inc(xtok_ready, 1)
                    if s == 0 and not (isinstance(g, int) and g == 0):
                        act.wait_ge(wscaled_ready, g + 1)
                        act.wait_ge(out_psum, CH * u)
                        split_high(O_, w_scaled)
                if last_pair(cur) and s >= 1:
                    mixer_std(s - 1)
                if i is not None:
                    row_std(i)
                if nxt:
                    gn, sn = nxt
                    n = NS * gn + sn
                    act.wait_ge(bT_psum, n + 1)
                    nc.scalar.copy(bT[:], ps[0][:]).then_inc(bT_ready, 1)
                    next_weights(B_)
                    act.wait_ge(cT_psum, n + 1)
                    wait(act, cdec_ready, n)
                    nc.scalar.copy(cT[:], ps[1][:]).then_inc(cT_ready, 1)
                    next_weights(C_)
                if i is not None:
                    hT_high(i, 0)
                    hT_high(i, 1)
                if cur:
                    act.wait_ge(y_ready, u + 1)
                    nc.scalar.copy(y_hi[:, 0, :], y_raw[:]).then_inc(yhi_ready, 1)
                    wait(act, ystats_done, 2 * u)
                    nc.scalar.activation(y_sq[:], y_raw[:], ACT.Square).then_inc(ysq_ready, 1)
                if nxt:
                    act.wait_ge(xT_psum, n + 1)
                    wait(act, y_skip, n)
                    nc.scalar.copy(xT[:], ps[0][:]).then_inc(xT_ready, 1)
                    next_weights(X_)
                    if first_pair(nxt):
                        act.wait_ge(ncum_pair_ready, sn + 1)
                    elif sn == 0:
                        act.wait_ge(ncum_pair_ready, NS + gn)
                    for a in range(2):
                        act.wait_ge(decay_psum, 3 * n + a + 1)
                        for c in range(CH):
                            part = slice(c * P, (c + 1) * P)
                            ins = nc.scalar.activation(dec[:, a, part], ps[2 + a][:, part], ACT.Exp,
                                                       bias=ncum_pair[:, CH * sn + c, a:a + 1])
                        ins.then_inc(decay_ready, 1)
                    act.wait_ge(decay_psum, 3 * n + 3)
                    nc.scalar.activation(e_cum[:], ps[4][:], ACT.Exp).then_inc(ecum_ready, 1)
                if i is not None:
                    hT_high(i, 2)
                    hT_high(i, 3)
                if nxt:
                    act.wait_ge(zT_psum, n + 1)
                    wait(act, y_ready, n)
                    nc.scalar.activation(gate[:], ps[1][:], ACT.Tanh, scale=0.5).then_inc(tanh_ready, 1)
                    next_weights(Z_)
                if i is not None and i < NS:
                    exp_a(i)
                    decay_to_end(i)
            mixer(act, step)

            def mlp_split(g, j):
                act.wait_ge(raw_loaded[j], 16 * split_count(g, j))
                split_high(j, raw[j])
                act.wait_ge(w2_scaled, g + 1)
                split_high(2 + j, raw[2 + j])
            for g in range(2):
                mlp_split(g, g)

            def mlp_step(cur, nxt):
                if nxt:
                    g, s, j = nxt
                    v = NS * g + s
                    act.wait_ge(hid_psum, v + 1)
                    if s == 0:
                        act.wait_ge(b1_ready, g + 1)
                    wait(act, glo_ready, v - 1)
                    nc.scalar.activation(gelu[s % 2][:], ps[s % 2][:], ACT.Gelu, bias=b1_pair[:, j:j + 1])\
                        .then_inc(gelu_ready, 1)
                    wait(act, mlp_psum, CH * (v - 1))
                    act.wait_ge(gelu_ready, v + 1)
                    nc.scalar.copy(y_hi[:, s % 2, :], gelu[s % 2][:]).then_inc(ghi_ready, 1)
                if cur and cur[1] == NS - 1 and not (isinstance(cur[0], int) and cur[0] + 2 >= HG):
                    act.wait_ge(mlp_psum, CH * (NS * cur[0] + NS))
                    mlp_split(cur[0] + 2, cur[2])

            def tail(i):
                row_std(i)
                for k in range(KT):
                    hT_high(i, k)
                if i == NS + 2:
                    mixer_std(3)
            mlp(act, mlp_step, tail)

        @block.vector
        def _(dve):
            chain = [0]

            def link(ins):
                chain[0] += 1
                ins.then_inc(dve_chain, 1)
                dve.wait_ge(dve_chain, chain[0])

            dve.wait_ge(silu_exp, 1)
            link(nc.vector.tensor_scalar(cc[:, 1, :], cc[:, 1, :], 1.0, None, ALU.add))
            link(nc.vector.reciprocal(cc[:, 2, :], cc[:, 1, :]))
            link(nc.vector.tensor_tensor(cc[:, 3, :], cc[:, 0, :], cc[:, 2, :], ALU.mult))
            dve.wait_ge(consts_made, 1)
            for k in range(KT):
                nc.vector.tensor_scalar(silu_b[:, k, :], ones[:], cc[:, 3, k:k + 1], None, ALU.mult)\
                    .then_inc(silu_ready, 1)

            def modulation(j):
                dve.wait_ge(mod_psum, j + 1)
                bank = ps[2 + j % 4]
                if j in (2, 5):
                    dst, sign = (gate_a if j == 2 else gate_b), y_raw
                    link(nc.vector.tensor_scalar(sign[:], bank[:], 0.0, 2.0, ALU.is_ge, ALU.mult))
                    link(nc.vector.tensor_scalar(sign[:], sign[:], -1.0, None, ALU.add))
                    nc.vector.tensor_tensor(dst[:], sign[:], bank[:], ALU.mult).then_inc(mod_ready, 1)
                    dve.wait_ge(mod_ready, j + 1)
                    link(nc.vector.scalar_tensor_tensor(dst[:], dst[:], 0.25, sign[:], ALU.max, ALU.mult))
                else:
                    nc.vector.tensor_scalar(mod_row[(j if j < 2 else j - 1)][:, :], bank[:],
                                            float(j in (1, 4)), None, ALU.add).then_inc(mod_ready, 1)

            def modulation_columns(v):
                dve.wait_ge(modcol_psum, v + 1)
                nc.vector.tensor_copy(mod_col[:, 2 * KT * v:2 * KT * (v + 1), :],
                                      ps[1][:, 4 * KT * v:4 * KT * (v + 1)].rearrange("p (v n) -> p v n", n=2))\
                    .then_inc(modcol_ready, 1)

            def newton(var, std, r, t):
                link(nc.vector.reciprocal(r, std))
                link(nc.vector.tensor_tensor(t, r, r, ALU.mult))
                link(nc.vector.tensor_tensor(t, t, var, ALU.mult))
                link(nc.vector.tensor_scalar(t, t, -0.5, 1.5, ALU.mult, ALU.add))
                link(nc.vector.tensor_tensor(r, r, t, ALU.mult))

            def row_stats(i):
                if i < NS:
                    wait_x(dve, i)
                for c in range(CH):
                    link(nc.vector.bn_stats(bst[:, c, :], x_buf(i)[:, c, :]))
                    link(nc.vector.bn_aggr(mv[:, c, :], bst[:, c, :]))
                nc.vector.tensor_scalar(rs[:, 0, 0:CH], mv[:, :, 1], EPS, None, ALU.add)\
                    .then_inc(var_ready, 1)

            def norm_rows(i):
                dve.wait_ge(std_ready, i + 1)
                newton(rs[:, 0, 0:CH], rs[:, 1, 0:CH], rs[:, 2, 0:CH], rs[:, 3, 0:CH])
                wait(dve, acc_set, CH * (i - NS + 1))
                for c in range(CH):
                    row = x_buf(i)[:, c, :]
                    nc.vector.tensor_scalar(row, row, mv[:, c, 0:1], rs[:, 2, c:c + 1],
                                            ALU.subtract, ALU.mult).then_inc(xn_ready, 1)

            def modulate(i, ks):
                vec = 0 if i < NS else 2 * KT
                for k in ks:
                    n = KT * i + k + 1
                    dve.wait_ge(xnT_psum, n)
                    if i < NS:
                        wait(dve, hlo_ready, n - KT)
                        wait(dve, a_psum, i)
                    else:
                        wait(dve, hlo_ready, n - 2 if n - 2 > KT * NS else 0)
                        dve.wait_ge(wlo_ready[O_], PAIRS)
                    nc.vector.tensor_scalar(h_raw(i, k)[:, :], ps[6 + k % 2][:], mod_col[:, vec + KT + k, 0:1],
                                            mod_col[:, vec + k, 0:1], ALU.mult, ALU.add)\
                        .then_inc(hraw_ready, 1)

            def cumulate(i):
                dve.wait_ge(ea_ready, i + 1)
                wait(dve, crows_stored, 16 * i)
                for c in range(CH):
                    part = slice(c * P, (c + 1) * P)
                    nc.vector.tensor_tensor_scan(cum_r[:, part], ones[0:HEADS, :], ea[:, part], 0.0,
                                                 ALU.mult, ALU.subtract).then_inc(cum_ready, 1)
                dve.wait_ge(cum_ready, CH * (i + 1))
                for c in range(CH):
                    part, last = slice(c * P, (c + 1) * P), (c + 1) * P - 1
                    ins = nc.vector.tensor_scalar(ea[:, part], cum_r[:, part], cum_r[:, last:last + 1],
                                                  None, ALU.subtract)
                ins.then_inc(wend_arg, 1)
                link(nc.vector.tensor_copy(parts[:, 0, :], cum_r))
                dve.wait_ge(hlo_ready, KT * (i + 1))
                link(nc.vector.tensor_tensor(rest, cum_r, parts[:, 0, :], ALU.subtract))
                link(nc.vector.tensor_copy(parts[:, 1, :], rest))
                nc.vector.tensor_tensor(parts[:, 2, :], rest, parts[:, 1, :], ALU.subtract)\
                    .then_inc(parts_ready, 1)

            def decay_columns(i):
                dve.wait_ge(cols_psum, i + 1)
                chunks = slice(CH * i, CH * (i + 1))
                cum_c = ps[7][:, 0:P].rearrange("p (c h) -> p c h", c=CH)
                nc.vector.tensor_scalar(ncum[:, chunks, :], cum_c, -1.0, None, ALU.mult)\
                    .then_inc(cols_ready, 1)
                nc.vector.tensor_scalar(ncum_pair[:, chunks, :], cum_c[:, :, 0:2], -1.0, None, ALU.mult)\
                    .then_inc(ncum_pair_ready, 1)
                nc.vector.tensor_copy(w_end[:, chunks, :], ps[7][:, P:2 * P].rearrange("p (c h) -> p c h", c=CH))\
                    .then_inc(cols_ready, 1)

            row_stats(0)
            modulation(0)
            modulation(1)
            modulation_columns(0)
            norm_rows(0)
            dve.wait_ge(modcol_ready, 1)
            modulate(0, range(KT))
            cumulate(0)
            modulation(2)
            for j in range(3, 6):
                modulation(j)
            dve.wait_ge(const_loaded, 16 * 6)
            nc.vector.tensor_tensor(gb_b2[:], gate_b[:], b2_row[:], ALU.mult).then_inc(modcol_ready, 1)
            modulation_columns(1)
            decay_columns(0)

            def scale_output_weights(g):
                gm, bt = gamma_c[:, bass.ds(g, 1)], beta_c[:, bass.ds(g, 1)]
                dve.wait_ge(raw_loaded[O_], 16 * (g + 1))
                if not (isinstance(g, int) and g == 0):
                    dve.wait_ge(wlo_ready[O_], g)
                    dve.wait_ge(wsums_step, 2 * g)
                nc.vector.scalar_tensor_tensor(wg_sum[:], raw[O_][:], gm, wg_sum[:], ALU.mult, ALU.add)\
                    .then_inc(wsums_step, 1)
                nc.vector.scalar_tensor_tensor(wb_sum[:], raw[O_][:], bt, wb_sum[:], ALU.mult, ALU.add)\
                    .then_inc(wsums_step, 1)
                nc.vector.scalar_tensor_tensor(w_scaled[:], raw[O_][:], gm, gate_a[:], ALU.mult, ALU.mult)\
                    .then_inc(wscaled_ready, 1)

            dve.wait_ge(zeroed, 5)
            scale_output_weights(0)
            row_stats(1)

            def pick_pair(g):
                nc.vector.tensor_scalar(ncum_pair[:], ncum[:, :, bass.ds(2 * g, 2)], 1.0, None, ALU.mult)\
                    .then_inc(ncum_pair_ready, 1)

            def mixer_stats(s):
                part = slice(CH * s, CH * (s + 1))
                dve.wait_ge(ystat_psum, s + 1)
                nc.vector.tensor_copy(yst[:, part, :], ps[6][:, 0:4 * CH].rearrange("p (t n) -> p t n", n=4))\
                    .then_inc(ystat_read, 1)
                dve.wait_ge(ystat_read, s + 1)
                mean, meansq = yst[:, part, 0], yst[:, part, 2]
                link(nc.vector.tensor_tensor(yv[:, 1, part], mean, mean, ALU.mult))
                link(nc.vector.tensor_tensor(yv[:, 0, part], meansq, yv[:, 1, part], ALU.subtract))
                link(nc.vector.tensor_scalar(yst[:, part, 3], mean, -1.0, None, ALU.mult))
                nc.vector.tensor_scalar(yv[:, 0, part], yv[:, 0, part], EPS, None, ALU.add)\
                    .then_inc(yvar_ready, 1)

            def mixer_rstd(s):
                part = slice(CH * s, CH * (s + 1))
                dve.wait_ge(ystd_ready, s + 1)
                newton(yv[:, 0, part], yv[:, 1, part], yv[:, 2, part], rs[:, 3, 0:CH])

            def residual(s):
                dve.wait_ge(wsums_ready, 2)
                for c in range(CH):
                    t = CH * s + c
                    row = x_buf(NS + s)[:, c, :]
                    link(nc.vector.scalar_tensor_tensor(acc[:, t, :], s1_row[:], yst[:, t, 3:4],
                                                        acc[:, t, :], ALU.mult, ALU.add))
                    dve.wait_ge(xb_ready, t + 1)
                    nc.vector.scalar_tensor_tensor(row, acc[:, t, :], yv[:, 2, t:t + 1], row,
                                                   ALU.mult, ALU.add).then_inc(x1_ready, 1)
                dve.wait_ge(x1_ready, CH * (s + 1))

            def add_out(u, s, c, first):
                dve.wait_ge(out_psum, CH * u + c + 1)
                row = acc[:, CH * s + c, :]
                if not first:
                    nc.vector.tensor_tensor(row, row, ps[6 + c % 2][:], ALU.add).then_inc(acc_added, 1)
                    return
                if s >= 2:
                    dve.wait_ge(hlo_ready, KT * NS)
                    dve.wait_ge(a_psum, NS)
                    dve.wait_ge(cols_psum, NS)
                    dve.wait_ge(crows_stored, 16 * NS)
                nc.vector.tensor_copy(row, ps[6 + c % 2][:]).then_inc(acc_added, 1)

            def step(cur, nxt):
                i = norm_at(cur, nxt)
                if cur:
                    g, s = cur
                    u = NS * g + s
                    dve.wait_ge(btok_psum, u + 1)
                    wv = w_end[:, CH * s:CH * (s + 1), bass.ds(2 * g, 2)]
                    nc.vector.tensor_tensor(b_tok[:].rearrange("p c (a n) -> p c a n", a=2),
                                            ps[5][:].rearrange("p (c a n) -> p c a n", c=CH, a=2),
                                            wv.unsqueeze(3).to_broadcast([P, CH, 2, HD]), ALU.mult)\
                        .then_inc(btok_ready, 1)
                    dve.wait_ge(scores_psum, u + 1)
                    for a in range(2):
                        dve.wait_ge(decay_ready, 2 * u + a + 1)
                        nc.vector.tensor_tensor(dec[:, a, :], dec[:, a, :], ps[2 + a][:], ALU.mult)\
                            .then_inc(mixed_ready, 1)
                    if s == NS - 1 and not (isinstance(g, int) and g + 1 >= PAIRS):
                        pick_pair(g + 1)
                if first_pair(nxt) and nxt[1]:
                    decay_columns(nxt[1])
                if last_pair(cur) and s >= 1:
                    mixer_rstd(s - 1)
                if i is not None:
                    norm_rows(i)
                if cur:
                    dve.wait_ge(dstate_psum, u + 1)
                    dve.wait_ge(ecum_ready, u + 1)
                    for c in range(CH):
                        t = CH * s + c
                        wait(dve, state_step, 8 * u + 2 * c)
                        for a in range(2):
                            rows_a, cols_a = slice(HD * a, HD * (a + 1)), slice(HD * a, HD * (a + 1))
                            new = state[rows_a, (t + 1) % 8, cols_a]
                            if t + 1 == NT:
                                nc.vector.memset(new, 0.0).then_inc(state_step, 1)
                            else:
                                nc.vector.scalar_tensor_tensor(
                                    new, state[rows_a, t % 8, cols_a],
                                    e_cum[rows_a, (c + 1) * P - 1:(c + 1) * P],
                                    ps[4][rows_a, c * P + HD * a:c * P + HD * (a + 1)],
                                    ALU.mult, ALU.add).then_inc(state_step, 1)
                if i is not None:
                    modulate(i, (0, 1))
                if cur:
                    dve.wait_ge(y_psum, u + 1)
                    dve.wait_ge(xT_ready, u + 1)
                    wait(dve, ylo_ready, u)
                    wait(dve, ystats_done, 2 * u)
                    nc.vector.scalar_tensor_tensor(y_raw[:], xT[:], skip_c[:, bass.ds(g, 1)], ps[5][:],
                                                   ALU.mult, ALU.add).then_inc(y_skip, 1)
                    dve.wait_ge(y_skip, u + 1)
                    dve.wait_ge(gate_ready, u + 1)
                    nc.vector.scalar_tensor_tensor(y_raw[:], y_raw[:], 0.5, gate[:], ALU.mult, ALU.mult)\
                        .then_inc(y_ready, 1)
                if i is not None:
                    modulate(i, (2, 3))
                if cur:
                    first = isinstance(g, int) and g == 0
                    add_out(u, s, 0, first)
                    add_out(u, s, 1, first)
                if nxt:
                    n = NS * nxt[0] + nxt[1]
                    dve.wait_ge(tanh_ready, n + 1)
                    nc.vector.scalar_tensor_tensor(gate[:], gate[:], 1.0, ps[1][:], ALU.add, ALU.mult)\
                        .then_inc(gate_ready, 1)
                if cur:
                    add_out(u, s, 2, first)
                    add_out(u, s, 3, first)
                    if s == NS - 1 and not (isinstance(g, int) and g + 1 >= PAIRS):
                        scale_output_weights(g + 1)
                if i is not None and i < NS:
                    cumulate(i)
                if last_pair(cur):
                    if s == 0:
                        dve.wait_ge(wsums_step, 2 * PAIRS)
                        for w in (wg_sum, wb_sum):
                            nc.vector.tensor_tensor(w[:], w[:], gate_a[:], ALU.mult).then_inc(wsums_scaled, 1)
                        for bank, row in ((6, s1_row), (7, beta_row)):
                            dve.wait_ge(wsums_psum, 1)
                            nc.vector.tensor_copy(row[:], ps[bank][:]).then_inc(wsums_ready, 1)
                    else:
                        residual(s - 1)
                if stats_at(cur, nxt) is not None:
                    row_stats(stats_at(cur, nxt))
                if last_pair(cur):
                    mixer_stats(s)
            mixer(dve, step)

            def mlp_scale(g, j):
                dve.wait_ge(raw_loaded[2 + j], 16 * split_count(g, j))
                nc.vector.tensor_tensor(raw[2 + j][:], raw[2 + j][:], gate_b[:], ALU.mult)\
                    .then_inc(w2_scaled, 1)
                wait(dve, gelu_ready, NS * (g - 1) if isinstance(g, int) and g >= 2 or not isinstance(g, int) else 0)
                nc.vector.tensor_scalar(b1_pair[:, j:j + 1], b1_c[:, bass.ds(g, 1)], 1.0, None, ALU.mult)\
                    .then_inc(b1_ready, 1)
            for g in range(2):
                mlp_scale(g, g)

            def tail(i):
                norm_rows(i)
                modulate(i, range(KT))
                if i == NS + 2:
                    mixer_rstd(3)
                    residual(3)
                    row_stats(i + 1)

            def mlp_step(cur, nxt):
                if cur:
                    g, s, j = cur
                    v = NS * g + s
                    if isinstance(g, int) and g == 0:
                        dve.wait_ge(acc_set, CH * (s + 1))
                    for c in range(CH):
                        dve.wait_ge(mlp_psum, CH * v + c + 1)
                        row = acc[:, CH * s + c, :]
                        nc.vector.tensor_tensor(row, row, ps[2 + c][:], ALU.add).then_inc(mlp_added, 1)
                    if s == 1 and not (isinstance(g, int) and g + 2 >= HG):
                        mlp_scale(g + 2, j)
            mlp(dve, mlp_step, tail)

        @block.tensor
        def _(pe):
            def three(bank, hi_l, lo_l, hi_r, lo_r, start, stop):
                nc.tensor.matmul(bank, lhsT=hi_l, rhs=hi_r, start=start, stop=False)
                nc.tensor.matmul(bank, lhsT=hi_l, rhs=lo_r, start=False, stop=False)
                return nc.tensor.matmul(bank, lhsT=lo_l, rhs=hi_r, start=False, stop=stop)

            def modulation(j):
                pe.wait_ge(wmod_loaded[j % 2], 16 * (j // 2 + 1))
                wait(pe, mod_ready, j - 3)
                for k in range(KT):
                    ins = nc.tensor.matmul(ps[2 + j % 4][:], lhsT=silu_b[:, k, :], rhs=w_mod_sb[:, j % 2, k, :],
                                           start=k == 0, stop=k == KT - 1)
                ins.then_inc(mod_psum, 1)

            def modulation_columns(v):
                pe.wait_ge(mod_ready, 3 * v + 2)
                for half in range(2):
                    for k in range(KT):
                        at = 2 * (KT * (2 * v + half) + k)
                        ins = nc.tensor.matmul(ps[1][:, at:at + 2], rhs=pick0[:], start=True, stop=True,
                                               lhsT=mod_row[2 * v + half][:, k * P:(k + 1) * P])
                ins.then_inc(modcol_psum, 1)

            def transpose_rows(i, ks):
                pe.wait_ge(xn_ready, CH * (i + 1))
                for k in ks:
                    if k >= 2:
                        pe.wait_ge(hraw_ready, KT * i + k - 1)
                    for c in range(CH):
                        ins = nc.tensor.transpose(ps[6 + k % 2][:, c * P:(c + 1) * P],
                                                  x_buf(i)[:, c, k * P:(k + 1) * P], ident[:])
                    ins.then_inc(xnT_psum, 1)

            def project_decays(i):
                pe.wait_ge(hraw_ready, KT * (i + 1))
                for k in range(KT):
                    ins = nc.tensor.matmul(ps[6][0:HEADS, :], lhsT=w_dec[:, k, :], rhs=h_raw(i, k)[:, :],
                                           start=k == 0, stop=k == KT - 1)
                ins.then_inc(a_psum, 1)

            def decay_columns(i):
                pe.wait_ge(cum_ready, CH * (i + 1))
                pe.wait_ge(wend_ready, i + 1)
                for j, src in enumerate((cum_r, ea)):
                    for c in range(CH):
                        at = j * P + c * HEADS
                        ins = nc.tensor.transpose(ps[7][:, at:at + HEADS], src[:, c * P:(c + 1) * P],
                                                  ident[0:HEADS, 0:HEADS])
                ins.then_inc(cols_psum, 1)

            pe.wait_ge(silu_ready, KT)
            pe.wait_ge(consts_made, 15)
            modulation(0)
            modulation(1)
            modulation_columns(0)
            transpose_rows(0, range(KT))
            pe.wait_ge(const_loaded, 16 * 6)
            project_decays(0)
            for j in range(2, 6):
                modulation(j)
            pe.wait_ge(modcol_ready, 1)
            modulation_columns(1)
            decay_columns(0)
            pe.wait_ge(modcol_ready, 3)
            pe.wait_ge(zeroed, 5)
            pe.wait_ge(mod_ready, 6)

            def project(m, g, s, bank, done):
                if m == B_ and isinstance(g, int) and g == 0:
                    pe.wait_ge(hlo_ready, KT * (s + 1))
                if s == 0:
                    pe.wait_ge(whi_ready[m], g + 1)
                    pe.wait_ge(wlo_ready[m], g + 1)
                tokens = slice(s * SUP, (s + 1) * SUP)
                for k in range(KT):
                    cols = slice(k * P, (k + 1) * P)
                    ins = three(ps[bank][:], w_hi[m][:, cols], w_lo[m][:, cols], hT_hi[:, k, tokens],
                                hT_lo[:, k, tokens], k == 0, k == KT - 1)
                ins.then_inc(done, 1)

            def step(cur, nxt):
                i = norm_at(cur, nxt)
                if cur:
                    g, s = cur
                    u = NS * g + s
                    pe.wait_ge(xT_ready, u + 1)
                    pe.wait_ge(ecum_ready, u + 1)
                    for c in range(CH):
                        part = slice(c * P, (c + 1) * P)
                        ins = nc.tensor.transpose(ps[4][:, part], xT[:, part], ident[:])
                    ins.then_inc(xtok_psum, 1)
                    pe.wait_ge(bT_ready, u + 1)
                    wait(pe, y_skip, u)
                    for c in range(CH):
                        part = slice(c * P, (c + 1) * P)
                        ins = nc.tensor.transpose(ps[5][:, part], bT[:, part], ident[:])
                    ins.then_inc(btok_psum, 1)
                    pe.wait_ge(cT_ready, u + 1)
                    pe.wait_ge(decay_ready, 2 * (u + 1))
                    for c in range(CH):
                        part = slice(c * P, (c + 1) * P)
                        for a in range(2):
                            head = slice(HD * a, HD * (a + 1))
                            ins = nc.tensor.matmul(ps[2 + a][:, part], lhsT=bT[head, part], rhs=cT[head, part],
                                                   start=True, stop=True)
                    ins.then_inc(scores_psum, 1)
                if nxt:
                    gn, sn = nxt
                    n = NS * gn + sn
                    wait(pe, xT_ready, n)
                    project(B_, gn, sn, 0, bT_psum)
                if first_pair(nxt) and sn:
                    pe.wait_ge(hraw_ready, KT * (sn + 1))
                    wait(pe, acc_added, CH * (n - 1))
                    decay_columns(sn)
                if cur:
                    pe.wait_ge(xtok_ready, u + 1)
                    pe.wait_ge(btok_ready, u + 1)
                    for c in range(CH):
                        ins = nc.tensor.matmul(ps[4][:, c * P:(c + 1) * P], lhsT=b_tok[:, c, :],
                                               rhs=x_tok[:, c, :], start=True, stop=True)
                    ins.then_inc(dstate_psum, 1)
                if nxt:
                    wait(pe, gate_ready, n)
                    project(C_, gn, sn, 1, cT_psum)
                if i is not None:
                    if i < NS:
                        pe.wait_ge(cols_ready, 2 * i)
                        pe.wait_ge(ea_ready, i)
                    else:
                        pe.wait_ge(ystat_read, cur[1])
                    if cur:
                        wait(pe, acc_added, CH * u)
                    transpose_rows(i, (0, 1))
                if cur:
                    pe.wait_ge(state_step, 8 * (u + 1))
                    pe.wait_ge(cdec_ready, u + 1)
                    for c in range(CH):
                        part = slice(c * P, (c + 1) * P)
                        nc.tensor.matmul(ps[5][:, part], lhsT=state[:, (CH * s + c) % 8, :], rhs=c_dec[:, part],
                                         start=c == 0, stop=False, skip_group_check=True)
                    pe.wait_ge(mixed_ready, 2 * (u + 1))
                    for c in range(CH):
                        part = slice(c * P, (c + 1) * P)
                        for a in range(2):
                            head = slice(HD * a, HD * (a + 1))
                            ins = nc.tensor.matmul(ps[5][head, part], lhsT=x_tok[:, c, head],
                                                   rhs=dec[:, a, part], start=False, stop=True,
                                                   skip_group_check=True)
                    ins.then_inc(y_psum, 1)
                if nxt:
                    pe.wait_ge(bT_ready, n + 1)
                    project(X_, gn, sn, 0, xT_psum)
                    pe.wait_ge(rows_loaded[sn % 2], 16 * (2 * gn + sn // 2 + 1))
                    wait(pe, mixed_ready, 2 * n)
                    wait(pe, state_step, 8 * n)
                    for a in range(2):
                        nc.tensor.matmul(ps[2 + a][:], lhsT=sel[:, a, :], rhs=rows[sn % 2][:], start=True,
                                         stop=False)
                        nc.tensor.matmul(ps[2 + a][:], lhsT=ident_b[:],
                                         rhs=causal[:].unsqueeze(1).to_broadcast([P, CH, P]), start=False,
                                         stop=True).then_inc(decay_psum, 1)
                    nc.tensor.matmul(ps[4][:], lhsT=sel[:, 2, :], rhs=rows[sn % 2][:], start=True, stop=True)\
                        .then_inc(decay_psum, 1)
                if i is not None:
                    transpose_rows(i, (2, 3))
                if nxt:
                    pe.wait_ge(cT_ready, n + 1)
                    project(Z_, gn, sn, 1, zT_psum)
                if i is not None and i < NS:
                    project_decays(i)
                if cur:
                    if first_pair(nxt):
                        pe.wait_ge(cols_ready, 2 * (sn + 1))
                    if i is not None:
                        pe.wait_ge(hraw_ready, KT * (i + 1))
                        if i < NS:
                            pe.wait_ge(ea_ready, i + 1)
                    elif last_pair(cur):
                        wait(pe, ystat_read, s)
                    pe.wait_ge(yhi_ready, u + 1)
                    pe.wait_ge(ylo_ready, u + 1)
                    if s == 0:
                        pe.wait_ge(whi_ready[O_], g + 1)
                        pe.wait_ge(wlo_ready[O_], g + 1)
                    for c in range(CH):
                        part = slice(c * P, (c + 1) * P)
                        wait(pe, acc_added, CH * u + c - 1)
                        three(ps[6 + c % 2][:], y_hi[:, 0, part], y_lo[:, 0, part], w_hi[O_][:], w_lo[O_][:],
                              True, True).then_inc(out_psum, 1)
                if last_pair(cur):
                    if s == 0:
                        pe.wait_ge(wsums_scaled, 2)
                        pe.wait_ge(acc_added, CH * (u + 1))
                        nc.tensor.matmul(ps[6][:], lhsT=ones[:], rhs=wg_sum[:], start=True, stop=True)
                        nc.tensor.matmul(ps[7][:], lhsT=ones[:], rhs=wb_sum[:], start=True, stop=True)\
                            .then_inc(wsums_psum, 1)
                        pe.wait_ge(wsums_ready, 2)
                    pe.wait_ge(acc_added, CH * (u + 1))
                    pe.wait_ge(ystats_done, 2 * (u + 1))
                    for c in range(CH):
                        part = slice(s * SUP + c * P, s * SUP + (c + 1) * P)
                        for at, sums in ((4 * c, y_sum), (4 * c + 2, yy_sum)):
                            ins = nc.tensor.matmul(ps[6][:, at:at + 2], lhsT=sums[:, part], rhs=mean_w[:],
                                                   start=True, stop=True)
                    ins.then_inc(ystat_psum, 1)
            mixer(pe, step)

            def tail(i):
                if i == NS + 2:
                    pe.wait_ge(ystat_read, NS)
                pe.wait_ge(hraw_ready, KT * i)
                transpose_rows(i, range(KT))

            def mlp_step(cur, nxt):
                if nxt:
                    g, s, j = nxt
                    v = NS * g + s
                    if s == 0:
                        pe.wait_ge(whi_ready[j], split_count(g, j))
                        pe.wait_ge(wlo_ready[j], split_count(g, j))
                    if isinstance(g, int) and g == 0:
                        pe.wait_ge(hlo_ready, KT * (NS + s + 1))
                    wait(pe, gelu_ready, v - 1)
                    tokens = slice(s * SUP, (s + 1) * SUP)
                    for k in range(KT):
                        cols = slice(k * P, (k + 1) * P)
                        ins = three(ps[s % 2][:], w_hi[j][:, cols], w_lo[j][:, cols], hT_hi[:, k, tokens],
                                    hT_lo[:, k, tokens], k == 0, k == KT - 1)
                    ins.then_inc(hid_psum, 1)
                if cur:
                    g, s, j = cur
                    v = NS * g + s
                    if s == 0:
                        pe.wait_ge(whi_ready[2 + j], split_count(g, j))
                        pe.wait_ge(wlo_ready[2 + j], split_count(g, j))
                    pe.wait_ge(ghi_ready, v + 1)
                    pe.wait_ge(glo_ready, v + 1)
                    for c in range(CH):
                        part = slice(c * P, (c + 1) * P)
                        wait(pe, mlp_added, CH * (v - 1) + c + 1)
                        three(ps[2 + c][:], y_hi[:, s % 2, part], y_lo[:, s % 2, part], w_hi[2 + j][:],
                              w_lo[2 + j][:], True, True).then_inc(mlp_psum, 1)
            mlp(pe, mlp_step, tail)


_OUT = "out_dram"


def kernel(**inputs):
    import numpy as _np
    import concourse.bacc as _bacc
    from concourse import mybir as _mybir
    from concourse.bass_utils import run_bass_kernel_spmd as _run

    def rows(name, *shape):
        return _np.asarray(inputs[name]).reshape(shape)

    def cols(name):
        return rows(name, -1, P).T

    def ktiles(w, n):
        return w.reshape(-1, n, KT, P).transpose(0, 3, 2, 1)

    w_in = _np.asarray(inputs["L0_attn_W_in"])
    main = ktiles(w_in[:4 * INNER], P).reshape(4, PAIRS, P, KT * P)[[2, 3, 0, 1]].transpose(1, 0, 2, 3)
    laid = {
        "x": rows("L0_attn_x", TOKENS, E),
        "w_pairs": main,
        "w_decay": ktiles(w_in[4 * INNER:], HEADS)[0],
        "w_out": _np.asarray(inputs["L0_attn_W_out"]).T.reshape(PAIRS, P, E),
        "gamma": cols("L0_attn_gamma"),
        "beta": cols("L0_attn_beta"),
        "skip": cols("L0_attn_D"),
        "w1": ktiles(_np.asarray(inputs["L0_ffn_proj1"]), P).reshape(HG, P, KT * P),
        "b1": cols("L0_ffn_proj1_bias"),
        "w2": _np.asarray(inputs["L0_ffn_proj2"]).T.reshape(HG, P, E),
        "b2": rows("L0_ffn_proj2_bias", E),
        "cond": cols("L0_c"),
        "w_mod": rows("L0_wmod", KT, P, 6, E).transpose(2, 1, 0, 3),
    }
    nc = _bacc.Bacc("TRN2", target_bir_lowering=False, num_devices=1)
    arrays, args = {}, {}
    for name, a in laid.items():
        a = _np.ascontiguousarray(a)
        arrays[f"{name}_dram"] = a
        args[name] = nc.dram_tensor(f"{name}_dram", a.shape, _mybir.dt.from_np(a.dtype), kind="ExternalInput").ap()
    args["out"] = nc.dram_tensor(_OUT, (TOKENS, E), F32, kind="ExternalOutput").ap()
    adaln_block(nc, **args)
    r = _run(nc, [arrays], core_ids=[0])
    return r.results[0][_OUT].reshape(1, TOKENS, E)
```

```python
from contextlib import ExitStack

import concourse.bass as bass
from concourse import mybir

ALU = mybir.AluOpType
ACT = mybir.ActivationFunctionType
F32 = mybir.dt.float32
F32R = mybir.dt.float32r

P = 128
TOKENS = 2048
E = 512
KT = E // P
HEADS = 32
HD = 64
INNER = HEADS * HD
PAIRS = INNER // P
SUP = 512
CH = SUP // P
NS = TOKENS // SUP
NT = TOKENS // P
HID = 2048
HG = HID // P
EPS = 1e-5
NEG = -1e30
B_, C_, X_, Z_, O_ = range(5)
OUT_BANK = (2, 3, 7, 6)


def adaln_block(nc, x, w_pairs, w_decay, w_out, gamma, beta, skip, w1, b1, w2, b2, cond, w_mod, out):
    cum_rows = nc.dram_tensor("cum_rows_scratch", (HEADS, TOKENS), F32, kind="Internal").ap()
    mod_rows = nc.dram_tensor("mod_rows_scratch", (4, E), F32, kind="Internal").ap()

    with ExitStack() as ctx:
        def sb(name, shape, dt=F32):
            return ctx.enter_context(nc.sbuf_tensor(name, shape, dt))

        def sem(name):
            return ctx.enter_context(nc.semaphore(name))

        ps = [ctx.enter_context(nc.psum_tensor(f"bank{i}", [P, 512], F32)) for i in range(8)]

        hT_hi = sb("hT_hi", [P, KT, TOKENS], F32R)
        hT_lo = sb("hT_lo", [P, KT, TOKENS], F32R)
        acc = sb("acc", [P, NT, E])
        y_sum = sb("y_sum", [P, TOKENS])
        yy_sum = sb("yy_sum", [P, TOKENS])
        raws = sb("raws", [P, 5, 512])
        raw = [raws[:, m, :] for m in range(5)]
        w_hi = [sb(f"w_hi{m}", [P, 512], F32R) for m in range(5)]
        w_lo = [sb(f"w_lo{m}", [P, 512], F32R) for m in range(5)]
        w_scaled = sb("w_scaled", [P, E])
        wg_sum = sb("wg_sum", [P, E])
        wb_sum = sb("wb_sum", [P, E])
        bT = sb("bT", [P, SUP])
        cT = sb("cT", [P, SUP])
        xT = sb("xT", [P, SUP])
        gate = sb("gate", [P, SUP])
        x_tok = sb("x_tok", [P, CH, P])
        b_tok = sb("b_tok", [P, CH, P])
        dec = sb("dec", [P, 2, SUP])
        e_cum = sb("e_cum", [P, SUP])
        c_dec = sb("c_dec", [P, SUP])
        state = sb("state", [P, 8, P])
        y_raw = sb("y_raw", [P, SUP])
        y_sq = sb("y_sq", [P, SUP])
        y_hi = sb("y_hi", [P, 2, SUP], F32R)
        y_lo = sb("y_lo", [P, 2, SUP], F32R)
        cum_b = [t[:, 1, :].bitcast(F32) for t in (y_hi, y_lo)]
        xin = sb("xin", [P, CH, E])
        gate_a = sb("gate_a", [P, E])
        gate_b = sb("gate_b", [P, E])
        gb_b2 = sb("gb_b2", [P, E])
        ncum = sb("ncum", [P, NT, HEADS])
        w_end = sb("w_end", [P, NT, HEADS])
        ncum_pair = sb("ncum_pair", [P, NT, 2])
        b1_pair = sb("b1_pair", [P, 2])
        ident = sb("ident", [P, P])
        causal = sb("causal", [P, P])
        ones = sb("ones", [P, P])
        mean_w = sb("mean_w", [P, 2])
        mod_col = sb("mod_col", [P, 4, KT])
        gamma_c = sb("gamma_c", [P, PAIRS])
        beta_c = sb("beta_c", [P, PAIRS])
        skip_c = sb("skip_c", [P, PAIRS])
        b1_c = sb("b1_c", [P, HG])
        cc = sb("cc", [P, 4, KT])
        bst = sb("bst", [P, CH, 6])
        mv = sb("mv", [P, CH, 2])
        rs = sb("rs", [P, 4, NT])
        yst = sb("yst", [P, NT, 4])
        yv = sb("yv", [P, 3, NT])
        w_mod_sb = acc[:, 0:8, :].rearrange("p (j k) e -> p j k e", j=2)
        h_raw1 = [acc[:, 8 + k, :] for k in range(KT)]
        ea = acc[0:HEADS, 12, :]
        cum_r = acc[0:HEADS, 13, :]
        w_dec = acc[:, 15, 384:512].rearrange("p (k h) -> p k h", k=KT)
        silu_b = dec[:, 0, :].rearrange("p (k m) -> p k m", k=KT)
        b2_row = gate
        gelu = [y_raw, y_sq]
        mod_row = [acc[0:1, 14, :], y_sq[0:1, :]]
        h_raw2 = [raw[O_], w_scaled, gate_a]
        s1_row, beta_row = wg_sum, wb_sum

        def h_raw(i, k):
            return h_raw1[k] if i < NS else h_raw2[k % 3]

        scan_tiles = [bT[:], cT[:], b_tok[:].rearrange("p c m -> p (c m)"), e_cum[:]], \
            [x_tok[:].rearrange("p c m -> p (c m)"), dec[:, 0, :], dec[:, 1, :], xT[:]]

        def x_row(i, c):
            if i >= NS + 2:
                return scan_tiles[i - NS - 2][c]
            return raws[:, c, :] if i == NS else xin[:, c, :]

        def norm_source(i, c):
            return x_row(i, c) if i < NS else acc[:, CH * (i - NS) + c, :]

        const_loaded = sem("const_loaded")
        cond_loaded = sem("cond_loaded")
        wmod_loaded = [sem(f"wmod_loaded{i}") for i in range(2)]
        x_loaded = [sem(f"x_loaded{i}") for i in range(4)]
        raw_loaded = [sem(f"raw_loaded{m}") for m in range(5)]
        cum_loaded = [sem(f"cum_loaded{a}") for a in range(2)]
        cum_stored = sem("cum_stored")
        out_stored = sem("out_stored")
        consts_made = sem("consts_made")
        silu_exp = sem("silu_exp")
        silu_ready = sem("silu_ready")
        mod_psum = sem("mod_psum")
        modrow_ready = sem("modrow_ready")
        mod_stored = sem("mod_stored")
        gate_row_ready = sem("gate_row_ready")
        modcol_ready = sem("modcol_ready")
        gb_b2_ready = sem("gb_b2_ready")
        dve_chain = sem("dve_chain")
        zeroed = sem("zeroed")
        var_ready = sem("var_ready")
        std_ready = sem("std_ready")
        rstd_ready = sem("rstd_ready")
        xn_ready = sem("xn_ready")
        xnT_psum = sem("xnT_psum")
        hraw_ready = sem("hraw_ready")
        hhi_ready = sem("hhi_ready")
        hlo_ready = sem("hlo_ready")
        ea_ready = sem("ea_ready")
        cum_ready = sem("cum_ready")
        wend_arg = sem("wend_arg")
        wend_ready = sem("wend_ready")
        cols_psum = sem("cols_psum")
        cols_ready = sem("cols_ready")
        whi_ready = [sem(f"whi_ready{m}") for m in range(5)]
        wlo_ready = [sem(f"wlo_ready{m}") for m in range(5)]
        wscaled_ready = sem("wscaled_ready")
        bT_psum, cT_psum, xT_psum, zT_psum = (sem(f"{n}T_psum") for n in "bcxz")
        bT_ready, cT_ready, xT_ready, tanh_ready = (sem(f"{n}_ready") for n in ("bT", "cT", "xT", "tanh"))
        gate_ready = sem("gate_ready")
        xtok_psum, btok_psum = sem("xtok_psum"), sem("btok_psum")
        xtok_ready, btok_ready = sem("xtok_ready"), sem("btok_ready")
        scores_psum = sem("scores_psum")
        decay_arg = sem("decay_arg")
        decay_ready = sem("decay_ready")
        ecum_ready = sem("ecum_ready")
        cdec_ready = sem("cdec_ready")
        mixed_ready = sem("mixed_ready")
        dstate_psum = sem("dstate_psum")
        state_step = sem("state_step")
        y_psum = sem("y_psum")
        y_skip = sem("y_skip")
        y_ready = sem("y_ready")
        yhi_ready = sem("yhi_ready")
        ylo_ready = sem("ylo_ready")
        ystats_done = sem("ystats_done")
        out_psum = sem("out_psum")
        acc_added = sem("acc_added")
        wsums_ready = sem("wsums_ready")
        xb_ready = sem("xb_ready")
        centered = sem("centered")
        x1_ready = sem("x1_ready")
        acc_set = sem("acc_set")
        w2_scaled = sem("w2_scaled")
        hid_psum = sem("hid_psum")
        gelu_ready = sem("gelu_ready")
        ghi_ready = sem("ghi_ready")
        glo_ready = sem("glo_ready")
        mlp_psum = sem("mlp_psum")
        mlp_added = sem("mlp_added")
        wsums_step = sem("wsums_step")
        ncum_pair_ready = sem("ncum_pair_ready")
        b1_ready = sem("b1_ready")
        wsums_scaled = sem("wsums_scaled")
        wsums_psum = sem("wsums_psum")
        ystat_psum = sem("ystat_psum")
        ystat_read = sem("ystat_read")
        yvar_ready = sem("yvar_ready")
        ystd_ready = sem("ystd_ready")
        ysq_ready = sem("ysq_ready")
        a_psum = sem("a_psum")

        def wait(eng, s, value):
            if not (isinstance(value, int) and value <= 0):
                eng.wait_ge(s, value)

        def after(g, s):
            return (g, s + 1) if s + 1 < NS else (g + 1, 0)

        def mixer(eng, step):
            step(None, (0, 0))
            for s in range(NS):
                step((0, s), after(0, s))
            with eng.Fori(1, PAIRS - 1) as g:
                for s in range(NS):
                    step((g, s), after(g, s))
            for s in range(NS):
                step((PAIRS - 1, s), after(PAIRS - 1, s) if s + 1 < NS else None)

        def mlp(eng, step):
            def pair(g0, last):
                for j in range(2):
                    for s in range(NS):
                        end = last and j == 1 and s + 1 == NS
                        nxt = (g0 + j, s + 1, j) if s + 1 < NS else (g0 + j + 1, 0, 1 - j)
                        step((g0 + j, s, j), None if end else nxt)
            first = [(j, s, j) for s in range(NS) for j in range(2)]
            for cur, nxt in zip([None] + first, first + [(2, 0, 0)]):
                step(cur, nxt)
            with eng.Fori(1, HG // 2 - 1) as r:
                pair(r * 2, False)
            pair(HG - 2, True)

        def first_round(unit):
            return unit is not None and isinstance(unit[0], int) and unit[0] < 2

        def place(unit):
            g, s, j = unit
            return 2 * s + j if first_round(unit) else NS * g + s

        def half(unit):
            return unit[2] if first_round(unit) else unit[1] % 2

        def mlp_norm_at(nxt):
            if first_round(nxt) and place(nxt) in (3, 5):
                return NS + 2 if place(nxt) == 3 else NS + 3
            return None

        def first_pair(nxt):
            return nxt is not None and isinstance(nxt[0], int) and nxt[0] == 0

        def last_pair(cur):
            return cur is not None and isinstance(cur[0], int) and cur[0] == PAIRS - 1

        def norm_at(cur, nxt):
            if first_pair(nxt) and nxt[1] + 1 < NS:
                return nxt[1] + 1
            if last_pair(cur) and cur[1] >= 2:
                return NS + cur[1] - 2
            return None

        def rows_normed_at(cur, nxt):
            return cur is not None and norm_at(cur, nxt) is not None

        def stats_bank(s):
            return 0 if s + 1 < NS else 5

        def wait_x(eng, i):
            if i >= NS + 2:
                eng.wait_ge(x_loaded[i - NS], 16 * CH)
            elif i == NS:
                eng.wait_ge(x_loaded[1], 16)
            else:
                eng.wait_ge(x_loaded[0], 16 * (i + 1 if i < NS else i))

        def split_count(g, j):
            return PAIRS + (g - j) // 2 + 1

        x_rows = x.rearrange("(s c p) e -> s p c e", p=P, c=CH)
        out_rows = out.rearrange("(s c p) e -> s p c e", p=P, c=CH)

        block = ctx.enter_context(nc.Block())

        @block.sync
        def _(sp):
            sp.dma_start(cc[:, 0, :], cond).then_inc(cond_loaded, 16)
            sp.dma_start(w_mod_sb[:, 0], w_mod[0]).then_inc(wmod_loaded[0], 16)
            sp.dma_start(xin[:], x_rows[0]).then_inc(x_loaded[0], 16)
            sp.dma_start(w_mod_sb[:, 1], w_mod[1]).then_inc(wmod_loaded[1], 16)
            sp.dma_start(w_dec, w_decay).then_inc(const_loaded, 16)
            for m in (B_, C_):
                sp.dma_start(raw[m], w_pairs[0, m]).then_inc(raw_loaded[m], 16)
            for dst, src in ((gamma_c, gamma), (beta_c, beta), (skip_c, skip), (b1_c, b1)):
                sp.dma_start(dst[:], src).then_inc(const_loaded, 16)
            sp.dma_start(b2_row[:], b2.partition_broadcast(P)).then_inc(const_loaded, 16)
            for m in (X_, Z_):
                sp.dma_start(raw[m], w_pairs[0, m]).then_inc(raw_loaded[m], 16)
            sp.dma_start(raw[O_], w_out[0]).then_inc(raw_loaded[O_], 16)

            def load_mod(j):
                sp.wait_ge(mod_psum, j - 1)
                sp.dma_start(w_mod_sb[:, j % 2], w_mod[j]).then_inc(wmod_loaded[j % 2], 16)

            def mod_columns(first):
                for v in (first, first + 1):
                    sp.wait_ge(modrow_ready, v + 1)
                    sp.dma_start(mod_rows[v:v + 1, :], mod_row[v % 2]).then_inc(mod_stored, 16)
                sp.wait_ge(mod_stored, 16 * (first + 2))
                for v in (first, first + 1):
                    with nc.allow_non_contiguous_dma(reason="512 elements, once"):
                        sp.dma_start(mod_col[:, v, :], mod_rows[v].rearrange("(k p) -> p k", p=P))\
                            .then_inc(modcol_ready, 16)

            mod_columns(0)
            load_mod(2)
            load_mod(3)
            sp.wait_ge(xnT_psum, KT)
            sp.dma_start(xin[:], x_rows[1]).then_inc(x_loaded[0], 16)
            load_mod(4)
            load_mod(5)

            def store_rows(i):
                sp.wait_ge(cum_ready, CH * (i + 1))
                sp.dma_start(cum_rows[:, i * SUP:(i + 1) * SUP], cum_r).then_inc(cum_stored, 16)

            store_rows(0)
            mod_columns(2)

            def step(cur, nxt):
                if nxt:
                    g, s = nxt
                    n = NS * g + s
                    if first_pair(nxt):
                        sp.wait_ge(cum_stored, 16 * (s + 1))
                    wait(sp, decay_arg, 2 * n)
                    wait(sp, ecum_ready, 2 * n)
                    for a in range(2):
                        src = cum_rows[bass.ds(2 * g + a, 1), s * SUP:(s + 1) * SUP]
                        sp.dma_start(cum_b[a], src.rearrange("a n -> (a n)").partition_broadcast(P))\
                            .then_inc(cum_loaded[a], 16)
                if cur and cur[1] == 0 and not (isinstance(cur[0], int) and cur[0] + 1 >= PAIRS):
                    g = cur[0] + 1
                    for m in range(5):
                        sp.wait_ge(wlo_ready[m] if m < O_ else wscaled_ready, g)
                        src = w_pairs[bass.ds(g, 1), m] if m < O_ else w_out[bass.ds(g, 1)]
                        sp.dma_start(raw[m], src.rearrange("a p n -> (a p) n"))\
                            .then_inc(raw_loaded[m], 16)
                if last_pair(cur) and cur[1] == 0:
                    for m in range(4):
                        sp.wait_ge(wlo_ready[m], PAIRS)
                    for i in (NS, NS + 1):
                        sp.dma_start(xin[:] if i > NS else raws[:, 0:CH, :], x_rows[i - NS])\
                            .then_inc(x_loaded[i == NS], 16)
                i = norm_at(cur, nxt)
                if i is not None and i < NS - 1:
                    sp.wait_ge(xnT_psum, KT * (i + 1))
                    sp.dma_start(xin[:], x_rows[i + 1]).then_inc(x_loaded[0], 16)
                if i == NS:
                    sp.wait_ge(xnT_psum, KT * (i + 1))
                    for g in range(2):
                        sp.dma_start(raw[g], w1[g]).then_inc(raw_loaded[g], 16)
                        sp.dma_start(raw[2 + g], w2[g]).then_inc(raw_loaded[2 + g], 16)
                if first_pair(nxt) and nxt[1] + 1 < NS:
                    store_rows(nxt[1] + 1)
            mixer(sp, step)
            units = NS * PAIRS
            uses = [(scores_psum, units), (cdec_ready, units), (dstate_psum, units), (state_step, 8 * units)], \
                [(y_psum, units), (y_psum, units), (y_psum, units), (y_skip, units)]
            for i in (NS + 2, NS + 3):
                for c in range(CH):
                    sp.wait_ge(*uses[i - NS - 2][c])
                    sp.dma_start(x_row(i, c), x_rows[i - NS, :, c, :]).then_inc(x_loaded[i - NS], 16)

            def mlp_step(cur, nxt):
                if cur and cur[1] == 0 and not (isinstance(cur[0], int) and cur[0] + 2 >= HG):
                    g, _, j = cur
                    for m, src in ((j, w1), (2 + j, w2)):
                        sp.wait_ge(wlo_ready[m], split_count(g, j))
                        sp.dma_start(raw[m], src[bass.ds(g + 2, 1)].rearrange("a p n -> (a p) n"))\
                            .then_inc(raw_loaded[m], 16)
                if cur and isinstance(cur[0], int) and cur[0] == HG - 1:
                    s = cur[1]
                    sp.wait_ge(mlp_added, CH * (NS * cur[0] + s + 1))
                    sp.dma_start(out_rows[s], acc[:, CH * s:CH * (s + 1), :]).then_inc(out_stored, 16)
            mlp(sp, mlp_step)
            sp.wait_ge(out_stored, 16 * NS)

        @block.gpsimd
        def _(pool):
            for t, value in ((ones, 1.0), (ident, 0.0), (causal, 0.0), (mean_w, 1.0 / INNER)):
                nc.gpsimd.memset(t[:], value).then_inc(consts_made, 1)
            pool.wait_ge(consts_made, 4)
            nc.gpsimd.affine_select(out=ident[:], in_=ident[:], compare_op=ALU.not_equal, fill=1.0, base=0,
                                    pattern=[[-1, P]], channel_multiplier=1).then_inc(consts_made, 1)
            nc.gpsimd.affine_select(out=causal[:], in_=causal[:], compare_op=ALU.is_ge, fill=NEG, base=0,
                                    pattern=[[1, P]], channel_multiplier=-1).then_inc(consts_made, 1)
            for t in (wg_sum, wb_sum, y_sum, yy_sum, state):
                nc.gpsimd.memset(t[:], 0.0).then_inc(zeroed, 1)

            def hT_low(i, k):
                tokens = slice(i % NS * SUP, (i % NS + 1) * SUP)
                pool.wait_ge(hraw_ready, KT * i + k + 1)
                pool.wait_ge(hhi_ready, KT * i + k + 1)
                nc.gpsimd.tensor_tensor(hT_lo[:, k, tokens], h_raw(i, k)[:, :], hT_hi[:, k, tokens].bitcast(F32),
                                        ALU.subtract).then_inc(hlo_ready, 1)

            def split_low(m, source, count):
                pool.wait_ge(whi_ready[m], count)
                nc.gpsimd.tensor_tensor(w_lo[m][:], source[:, :], w_hi[m][:].bitcast(F32), ALU.subtract)\
                    .then_inc(wlo_ready[m], 1)

            for k in range(KT):
                hT_low(0, k)
            for m in range(5):
                split_low(m, raw[m] if m < O_ else w_scaled, 1)

            def add_beta_row(i):
                wait_x(pool, i)
                pool.wait_ge(wsums_ready, 2)
                for c in range(CH):
                    row = x_row(i, c)
                    nc.gpsimd.tensor_tensor(row, row, beta_row[:], ALU.add).then_inc(xb_ready, 1)

            def step(cur, nxt):
                more = nxt and nxt[1] == NS - 1 and not (isinstance(nxt[0], int) and nxt[0] + 1 >= PAIRS)
                i = norm_at(cur, nxt)
                if cur:
                    g, s = cur
                    u = NS * g + s
                    pool.wait_ge(ecum_ready, 2 * (u + 1))
                    pool.wait_ge(cT_ready, u + 1)
                    nc.gpsimd.tensor_tensor(c_dec[:], cT[:], e_cum[:], ALU.mult).then_inc(cdec_ready, 1)
                    if s == 0 and not (isinstance(g, int) and g == 0):
                        split_low(O_, w_scaled, g + 1)
                if more:
                    split_low(B_, raw[B_], nxt[0] + 2)
                    split_low(C_, raw[C_], nxt[0] + 2)
                if cur:
                    tokens = slice(s * SUP, (s + 1) * SUP)
                    if last_pair(cur) and s + 1 == NS:
                        for m in range(4):
                            split_low(m, raw[m], split_count(m % 2, m % 2))
                    pool.wait_ge(y_ready, u + 1)
                    pool.wait_ge(yhi_ready, u + 1)
                    nc.gpsimd.tensor_tensor(y_lo[:, 0, :], y_raw[:], y_hi[:, 0, :].bitcast(F32),
                                            ALU.subtract).then_inc(ylo_ready, 1)
                    if i is not None:
                        hT_low(i, 0)
                    wait(pool, ystats_done, 2 * u)
                    nc.gpsimd.tensor_tensor(y_sum[:, tokens], y_sum[:, tokens], y_raw[:], ALU.add)\
                        .then_inc(ystats_done, 1)
                    pool.wait_ge(ysq_ready, u + 1)
                    nc.gpsimd.tensor_tensor(yy_sum[:, tokens], yy_sum[:, tokens], y_sq[:], ALU.add)\
                        .then_inc(ystats_done, 1)
                if i is not None:
                    for k in range(0 if cur is None else 1, KT):
                        hT_low(i, k)
                if more:
                    split_low(X_, raw[X_], nxt[0] + 2)
                    split_low(Z_, raw[Z_], nxt[0] + 2)
                if last_pair(cur) and s <= 1:
                    add_beta_row(NS + s)
            mixer(pool, step)

            def mlp_step(cur, nxt):
                turn = cur and cur[1] == NS - 1 and not (isinstance(cur[0], int) and cur[0] + 2 >= HG)
                if turn:
                    split_low(cur[2], raw[cur[2]], split_count(cur[0] + 2, cur[2]))
                i = mlp_norm_at(nxt)
                if i is not None:
                    for k in range(KT):
                        hT_low(i, k)
                if nxt:
                    v, b = place(nxt), half(nxt)
                    pool.wait_ge(gelu_ready, v + 1)
                    pool.wait_ge(ghi_ready, v + 1)
                    nc.gpsimd.tensor_tensor(y_lo[:, b, :], gelu[b][:], y_hi[:, b, :].bitcast(F32),
                                            ALU.subtract).then_inc(glo_ready, 1)
                if first_round(nxt) and place(nxt) == 1:
                    pool.wait_ge(xb_ready, CH * (NS - 1))
                    add_beta_row(NS + 3)
                if turn:
                    split_low(2 + cur[2], raw[2 + cur[2]], split_count(cur[0] + 2, cur[2]))
            mlp(pool, mlp_step)

        @block.scalar
        def _(act):
            act.wait_ge(cond_loaded, 16)
            nc.scalar.activation(cc[:, 1, :], cc[:, 0, :], ACT.Exp, scale=-1.0).then_inc(silu_exp, 1)

            def hT_high(i, k):
                tokens = slice(i % NS * SUP, (i % NS + 1) * SUP)
                act.wait_ge(hraw_ready, KT * i + k + 1)
                nc.scalar.copy(hT_hi[:, k, tokens], h_raw(i, k)[:, :]).then_inc(hhi_ready, 1)

            def norm_rows(i):
                act.wait_ge(rstd_ready, i + 1)
                for c in range(CH):
                    nc.scalar.activation(x_row(i, c), norm_source(i, c), ACT.Identity, bias=rs[:, 3, c:c + 1],
                                         scale=rs[:, 2, c:c + 1]).then_inc(xn_ready, 1)

            def modulate(i, ks):
                vec = 0 if i < NS else 2
                for k in ks:
                    n = KT * i + k + 1
                    act.wait_ge(xnT_psum, n)
                    if i < NS:
                        wait(act, hlo_ready, n - KT)
                        wait(act, a_psum, i)
                    else:
                        act.wait_ge(hlo_ready, KT * i + (k == 3))
                        act.wait_ge(wlo_ready[O_], PAIRS)
                        act.wait_ge(modcol_ready, 16 * 4)
                        act.wait_ge(wsums_scaled, 2)
                    nc.scalar.activation(h_raw(i, k)[:, :], ps[6 + k % 2][:], ACT.Identity,
                                         bias=mod_col[:, vec, k:k + 1], scale=mod_col[:, vec + 1, k:k + 1])\
                        .then_inc(hraw_ready, 1)
                    hT_high(i, k)

            def row_std(i):
                act.wait_ge(var_ready, i + 1)
                nc.scalar.activation(rs[:, 1, 0:CH], rs[:, 0, 0:CH], ACT.Sqrt).then_inc(std_ready, 1)

            def mixer_std(s):
                act.wait_ge(yvar_ready, s + 1)
                part = slice(CH * s, CH * (s + 1))
                nc.scalar.activation(yv[:, 1, part], yv[:, 0, part], ACT.Sqrt).then_inc(ystd_ready, 1)

            def exp_a(i):
                act.wait_ge(a_psum, i + 1)
                nc.scalar.activation(ea, ps[6][0:HEADS, :], ACT.Exp).then_inc(ea_ready, 1)

            def decay_to_end(i):
                act.wait_ge(wend_arg, i + 1)
                nc.scalar.activation(ea, ea, ACT.Exp, scale=-1.0).then_inc(wend_ready, 1)

            def split_high(m, source):
                nc.scalar.copy(w_hi[m][:], source[:, :]).then_inc(whi_ready[m], 1)

            row_std(0)
            norm_rows(0)
            for k in range(KT):
                hT_high(0, k)
            for m in (B_, C_):
                act.wait_ge(raw_loaded[m], 16)
                split_high(m, raw[m])
            exp_a(0)
            decay_to_end(0)
            for m in (X_, Z_):
                act.wait_ge(raw_loaded[m], 16)
                split_high(m, raw[m])
            row_std(1)
            norm_rows(1)
            act.wait_ge(wscaled_ready, 1)
            split_high(O_, w_scaled)

            def step(cur, nxt):
                more = nxt and nxt[1] == NS - 1 and not (isinstance(nxt[0], int) and nxt[0] + 1 >= PAIRS)

                def next_weights(m):
                    if more:
                        act.wait_ge(raw_loaded[m], 16 * (nxt[0] + 2))
                        split_high(m, raw[m])

                i = norm_at(cur, nxt)
                if cur:
                    g, s = cur
                    u = NS * g + s
                    act.wait_ge(xtok_psum, u + 1)
                    nc.scalar.copy(x_tok[:].rearrange("p c m -> p (c m)"), ps[4][:]).then_inc(xtok_ready, 1)
                    if s == 0 and not (isinstance(g, int) and g == 0):
                        act.wait_ge(wscaled_ready, g + 1)
                        act.wait_ge(out_psum, CH * u)
                        split_high(O_, w_scaled)
                if last_pair(cur) and s + 1 == NS:
                    for j in range(2):
                        act.wait_ge(raw_loaded[j], 16 * split_count(j, j))
                        split_high(j, raw[j])
                if rows_normed_at(cur, nxt):
                    row_std(i)
                if nxt:
                    gn, sn = nxt
                    n = NS * gn + sn
                    act.wait_ge(bT_psum, n + 1)
                    nc.scalar.copy(bT[:], ps[0][:]).then_inc(bT_ready, 1)
                    next_weights(B_)
                if rows_normed_at(cur, nxt):
                    norm_rows(i)
                if last_pair(cur) and s >= 1:
                    mixer_std(s - 1)
                if last_pair(cur) and s + 1 == NS:
                    for j in range(2):
                        act.wait_ge(w2_scaled, j + 1)
                        split_high(2 + j, raw[2 + j])
                if nxt:
                    act.wait_ge(cT_psum, n + 1)
                    wait(act, cdec_ready, n)
                    nc.scalar.copy(cT[:], ps[1][:]).then_inc(cT_ready, 1)
                    next_weights(C_)
                if cur:
                    act.wait_ge(y_ready, u + 1)
                    nc.scalar.copy(y_hi[:, 0, :], y_raw[:]).then_inc(yhi_ready, 1)
                    wait(act, ystats_done, 2 * u)
                    nc.scalar.activation(y_sq[:], y_raw[:], ACT.Square).then_inc(ysq_ready, 1)
                if i is not None:
                    modulate(i, (0, 1))
                if nxt:
                    act.wait_ge(xT_psum, n + 1)
                    wait(act, y_skip, n)
                    nc.scalar.copy(xT[:], ps[0][:]).then_inc(xT_ready, 1)
                    next_weights(X_)
                if i is not None:
                    modulate(i, (2, 3))
                if nxt:
                    wait(act, state_step, 8 * n)
                    wait(act, cdec_ready, n)
                    for a in range(2):
                        half = slice(HD * a, HD * (a + 1))
                        act.wait_ge(cum_loaded[a], 16 * (n + 1))
                        nc.scalar.activation(e_cum[half, :], cum_b[a][half, :], ACT.Exp).then_inc(ecum_ready, 1)
                if nxt:
                    for a in range(2):
                        act.wait_ge(decay_arg, 2 * n + a + 1)
                        nc.scalar.activation(dec[:, a, :], dec[:, a, :], ACT.Exp).then_inc(decay_ready, 1)
                if nxt:
                    act.wait_ge(zT_psum, n + 1)
                    wait(act, y_ready, n)
                    nc.scalar.activation(gate[:], ps[1][:], ACT.Tanh, scale=0.5).then_inc(tanh_ready, 1)
                    next_weights(Z_)
                if i is not None and i < NS:
                    exp_a(i)
                    decay_to_end(i)
            mixer(act, step)


            def mlp_step(cur, nxt):
                turn = cur and cur[1] == NS - 1 and not (isinstance(cur[0], int) and cur[0] + 2 >= HG)
                if turn:
                    act.wait_ge(hid_psum, place(cur) + 1)
                    act.wait_ge(raw_loaded[cur[2]], 16 * split_count(cur[0] + 2, cur[2]))
                    split_high(cur[2], raw[cur[2]])
                i = mlp_norm_at(nxt)
                if i is not None:
                    modulate(i, range(KT))
                if first_round(nxt) and place(nxt) == 4:
                    row_std(NS + 3)
                    norm_rows(NS + 3)
                if nxt:
                    g, _, j = nxt
                    v, b = place(nxt), half(nxt)
                    if cur is None:
                        act.wait_ge(ylo_ready, NS * PAIRS)
                        act.wait_ge(ystats_done, 2 * NS * PAIRS)
                    act.wait_ge(hid_psum, v + 1)
                    if nxt[1] == 0:
                        act.wait_ge(b1_ready, g + 1)
                    wait(act, glo_ready, v - 1)
                    nc.scalar.activation(gelu[b][:], ps[b][:], ACT.Gelu, bias=b1_pair[:, j:j + 1])\
                        .then_inc(gelu_ready, 1)
                    if cur is None:
                        act.wait_ge(out_psum, CH * NS * PAIRS)
                    wait(act, mlp_psum, CH * (v - 1))
                    act.wait_ge(gelu_ready, v + 1)
                    nc.scalar.copy(y_hi[:, b, :], gelu[b][:]).then_inc(ghi_ready, 1)
                if first_round(nxt) and place(nxt) == 1:
                    row_std(NS + 2)
                    mixer_std(3)
                    norm_rows(NS + 2)
                if turn:
                    act.wait_ge(mlp_psum, CH * (place(cur) + 1))
                    act.wait_ge(w2_scaled, cur[0] + 3)
                    split_high(2 + cur[2], raw[2 + cur[2]])
            mlp(act, mlp_step)

        @block.vector
        def _(dve):
            chain = [0]

            def link(*done):
                chain[0] += len(done)
                for ins in done:
                    ins.then_inc(dve_chain, 1)
                dve.wait_ge(dve_chain, chain[0])

            dve.wait_ge(silu_exp, 1)
            link(nc.vector.tensor_scalar(cc[:, 1, :], cc[:, 1, :], 1.0, None, ALU.add))
            link(nc.vector.reciprocal(cc[:, 2, :], cc[:, 1, :]))
            link(nc.vector.tensor_tensor(cc[:, 3, :], cc[:, 0, :], cc[:, 2, :], ALU.mult))
            dve.wait_ge(consts_made, 1)
            for k in range(KT):
                nc.vector.tensor_scalar(silu_b[:, k, :], ones[:], cc[:, 3, k:k + 1], None, ALU.mult)\
                    .then_inc(silu_ready, 1)

            def gate_row(v, dst):
                sign, bank = y_raw, ps[2 + v]
                dve.wait_ge(mod_psum, 3 * v + 3)
                link(nc.vector.tensor_scalar(sign[:], bank[:], 0.0, 2.0, ALU.is_ge, ALU.mult))
                link(nc.vector.tensor_scalar(sign[:], sign[:], -1.0, None, ALU.add))
                link(nc.vector.tensor_tensor(dst[:], sign[:], bank[:], ALU.mult))
                nc.vector.scalar_tensor_tensor(dst[:], dst[:], 0.25, sign[:], ALU.max, ALU.mult)\
                    .then_inc(gate_row_ready, 1)
                dve.wait_ge(gate_row_ready, v + 1)

            def modulation_row(v):
                dve.wait_ge(mod_psum, (1, 2, 4, 5)[v])
                if v >= 2:
                    dve.wait_ge(mod_stored, 16 * 2)
                nc.vector.tensor_scalar(mod_row[v % 2], ps[v % 2][0:1, :], float(v % 2), None, ALU.add)\
                    .then_inc(modrow_ready, 1)

            def newton(var, std, r, t):
                link(nc.vector.reciprocal(r, std))
                link(nc.vector.tensor_tensor(t, r, r, ALU.mult))
                link(nc.vector.tensor_tensor(t, t, var, ALU.mult))
                link(nc.vector.tensor_scalar(t, t, -0.5, 1.5, ALU.mult, ALU.add))
                link(nc.vector.tensor_tensor(r, r, t, ALU.mult))

            def row_stats(i):
                if i < NS:
                    wait_x(dve, i)
                else:
                    dve.wait_ge(x1_ready, CH * (i - NS + 1))
                link(*[nc.vector.bn_stats(bst[:, c, :], norm_source(i, c)) for c in range(CH)])
                link(*[nc.vector.bn_aggr(mv[:, c, :], bst[:, c, :]) for c in range(CH)])
                nc.vector.tensor_scalar(rs[:, 0, 0:CH], mv[:, :, 1], EPS, None, ALU.add)\
                    .then_inc(var_ready, 1)

            def row_rstd(i):
                dve.wait_ge(std_ready, i + 1)
                newton(rs[:, 0, 0:CH], rs[:, 1, 0:CH], rs[:, 2, 0:CH], rs[:, 3, 0:CH])
                nc.vector.scalar_tensor_tensor(rs[:, 3, 0:CH], mv[:, :, 0], -1.0, rs[:, 2, 0:CH],
                                               ALU.mult, ALU.mult).then_inc(rstd_ready, 1)

            def cumulate(i):
                dve.wait_ge(ea_ready, i + 1)
                if i:
                    dve.wait_ge(cum_stored, 16 * i)
                    dve.wait_ge(cols_psum, i)
                for c in range(CH):
                    part = slice(c * P, (c + 1) * P)
                    nc.vector.tensor_tensor_scan(cum_r[:, part], ones[0:HEADS, :], ea[:, part], 0.0,
                                                 ALU.mult, ALU.subtract).then_inc(cum_ready, 1)
                dve.wait_ge(cum_ready, CH * (i + 1))
                for c in range(CH):
                    part, last = slice(c * P, (c + 1) * P), (c + 1) * P - 1
                    ins = nc.vector.tensor_scalar(ea[:, part], cum_r[:, part], cum_r[:, last:last + 1],
                                                  None, ALU.subtract)
                ins.then_inc(wend_arg, 1)

            def decay_columns(i):
                dve.wait_ge(cols_psum, i + 1)
                chunks = slice(CH * i, CH * (i + 1))
                cum_c = ps[7][:, 0:P].rearrange("p (c h) -> p c h", c=CH)
                nc.vector.tensor_scalar(ncum[:, chunks, :], cum_c, -1.0, None, ALU.mult)\
                    .then_inc(cols_ready, 1)
                nc.vector.tensor_scalar(ncum_pair[:, chunks, :], cum_c[:, :, 0:2], -1.0, None, ALU.mult)\
                    .then_inc(ncum_pair_ready, 1)
                nc.vector.tensor_copy(w_end[:, chunks, :], ps[7][:, P:2 * P].rearrange("p (c h) -> p c h", c=CH))\
                    .then_inc(cols_ready, 1)

            row_stats(0)
            modulation_row(0)
            row_rstd(0)
            modulation_row(1)
            dve.wait_ge(modcol_ready, 16 * 2)
            for k in range(KT):
                dve.wait_ge(xnT_psum, k + 1)
                nc.vector.tensor_scalar(h_raw(0, k)[:, :], ps[6 + k % 2][:], mod_col[:, 1, k:k + 1],
                                        mod_col[:, 0, k:k + 1], ALU.mult, ALU.add).then_inc(hraw_ready, 1)
            gate_row(0, gate_a)
            cumulate(0)
            modulation_row(2)
            row_stats(1)
            decay_columns(0)
            modulation_row(3)
            row_rstd(1)
            gate_row(1, gate_b)
            dve.wait_ge(const_loaded, 16 * 6)
            nc.vector.tensor_tensor(gb_b2[:], gate_b[:], b2_row[:], ALU.mult).then_inc(gb_b2_ready, 1)

            def scale_output_weights(g):
                gm, bt = gamma_c[:, bass.ds(g, 1)], beta_c[:, bass.ds(g, 1)]
                dve.wait_ge(raw_loaded[O_], 16 * (g + 1))
                if not (isinstance(g, int) and g == 0):
                    dve.wait_ge(wlo_ready[O_], g)
                    dve.wait_ge(wsums_step, 2 * g)
                nc.vector.scalar_tensor_tensor(wg_sum[:], raw[O_][:], gm, wg_sum[:], ALU.mult, ALU.add)\
                    .then_inc(wsums_step, 1)
                nc.vector.scalar_tensor_tensor(wb_sum[:], raw[O_][:], bt, wb_sum[:], ALU.mult, ALU.add)\
                    .then_inc(wsums_step, 1)
                nc.vector.scalar_tensor_tensor(w_scaled[:], raw[O_][:], gm, gate_a[:], ALU.mult, ALU.mult)\
                    .then_inc(wscaled_ready, 1)

            def mlp_scale(g, j):
                dve.wait_ge(raw_loaded[2 + j], 16 * split_count(g, j))
                nc.vector.tensor_tensor(raw[2 + j][:], raw[2 + j][:], gate_b[:], ALU.mult)\
                    .then_inc(w2_scaled, 1)
                nc.vector.tensor_scalar(b1_pair[:, j:j + 1], b1_c[:, bass.ds(g, 1)], 1.0, None, ALU.mult)\
                    .then_inc(b1_ready, 1)

            def decay_args(g, s):
                n = NS * g + s
                dve.wait_ge(ncum_pair_ready, s + 1 if isinstance(g, int) and g == 0 else NS + g)
                for a in range(2):
                    dve.wait_ge(cum_loaded[a], 16 * (n + 1))
                    for c in range(CH):
                        part = slice(c * P, (c + 1) * P)
                        ins = nc.vector.scalar_tensor_tensor(dec[:, a, part], cum_b[a][:, part],
                                                             ncum_pair[:, CH * s + c, a:a + 1], causal[:],
                                                             ALU.add, ALU.min)
                    ins.then_inc(decay_arg, 1)

            dve.wait_ge(consts_made, 6)
            dve.wait_ge(zeroed, 5)
            scale_output_weights(0)

            def pick_pair(g):
                nc.vector.tensor_scalar(ncum_pair[:], ncum[:, :, bass.ds(2 * g, 2)], 1.0, None, ALU.mult)\
                    .then_inc(ncum_pair_ready, 1)

            def read_mixer_stats(s):
                part = slice(CH * s, CH * (s + 1))
                dve.wait_ge(ystat_psum, s + 1)
                nc.vector.tensor_copy(yst[:, part, :], ps[stats_bank(s)][:, 0:4 * CH].rearrange("p (t n) -> p t n", n=4))\
                    .then_inc(ystat_read, 1)

            def mixer_variance(s):
                part = slice(CH * s, CH * (s + 1))
                dve.wait_ge(ystat_read, s + 1)
                mean, meansq = yst[:, part, 0], yst[:, part, 2]
                link(nc.vector.tensor_tensor(yv[:, 1, part], mean, mean, ALU.mult),
                     nc.vector.tensor_scalar(yst[:, part, 3], mean, -1.0, None, ALU.mult))
                link(nc.vector.tensor_tensor(yv[:, 0, part], meansq, yv[:, 1, part], ALU.subtract))
                nc.vector.tensor_scalar(yv[:, 0, part], yv[:, 0, part], EPS, None, ALU.add)\
                    .then_inc(yvar_ready, 1)

            def mixer_rstd(s):
                part = slice(CH * s, CH * (s + 1))
                dve.wait_ge(ystd_ready, s + 1)
                newton(yv[:, 0, part], yv[:, 1, part], yv[:, 2, part], yst[:, part, 1])

            def center(s):
                dve.wait_ge(wsums_ready, 2)
                dve.wait_ge(acc_added, CH * (NS * (PAIRS - 1) + s + 1))
                for c in range(CH):
                    row = acc[:, CH * s + c, :]
                    nc.vector.scalar_tensor_tensor(row, s1_row[:], yst[:, CH * s + c, 3:4], row,
                                                   ALU.mult, ALU.add).then_inc(centered, 1)

            def add_beta_row(i):
                wait_x(dve, i)
                for c in range(CH):
                    nc.vector.tensor_tensor(x_row(i, c), x_row(i, c), beta_row[:], ALU.add).then_inc(xb_ready, 1)

            def residual(s):
                dve.wait_ge(centered, CH * (s + 1))
                for c in range(CH):
                    t = CH * s + c
                    dve.wait_ge(xb_ready, t + 1)
                    nc.vector.scalar_tensor_tensor(acc[:, t, :], acc[:, t, :], yv[:, 2, t:t + 1],
                                                   x_row(NS + s, c), ALU.mult, ALU.add).then_inc(x1_ready, 1)

            def add_out(u, s, c, first):
                dve.wait_ge(out_psum, CH * u + c + 1)
                row = acc[:, CH * s + c, :]
                if not first:
                    nc.vector.tensor_tensor(row, row, ps[OUT_BANK[c]][:], ALU.add).then_inc(acc_added, 1)
                    return
                if s >= 2:
                    dve.wait_ge(hlo_ready, KT * NS)
                    dve.wait_ge(a_psum, NS)
                    dve.wait_ge(cols_psum, NS)
                    dve.wait_ge(cum_stored, 16 * NS)
                nc.vector.tensor_copy(row, ps[OUT_BANK[c]][:]).then_inc(acc_added, 1)

            def step(cur, nxt):
                i = norm_at(cur, nxt)
                if cur:
                    g, s = cur
                    u = NS * g + s
                    if last_pair(cur) and s >= 1:
                        read_mixer_stats(s - 1)
                    dve.wait_ge(btok_psum, u + 1)
                    wv = w_end[:, CH * s:CH * (s + 1), bass.ds(2 * g, 2)]
                    nc.vector.tensor_tensor(b_tok[:].rearrange("p c (a n) -> p c a n", a=2),
                                            ps[5][:].rearrange("p (c a n) -> p c a n", c=CH, a=2),
                                            wv.unsqueeze(3).to_broadcast([P, CH, 2, HD]), ALU.mult)\
                        .then_inc(btok_ready, 1)
                    dve.wait_ge(scores_psum, u + 1)
                    for a in range(2):
                        dve.wait_ge(decay_ready, 2 * u + a + 1)
                        nc.vector.tensor_tensor(dec[:, a, :], dec[:, a, :], ps[2 + a][:], ALU.mult)\
                            .then_inc(mixed_ready, 1)
                    if s == NS - 1 and not (isinstance(g, int) and g + 1 >= PAIRS):
                        pick_pair(g + 1)
                if first_pair(nxt) and nxt[1]:
                    decay_columns(nxt[1])
                if last_pair(cur) and s == 0:
                    dve.wait_ge(wsums_step, 2 * PAIRS)
                    for w in (wg_sum, wb_sum):
                        nc.vector.tensor_tensor(w[:], w[:], gate_a[:], ALU.mult).then_inc(wsums_scaled, 1)
                if rows_normed_at(cur, nxt):
                    row_rstd(i)
                if cur:
                    dve.wait_ge(dstate_psum, u + 1)
                    dve.wait_ge(ecum_ready, 2 * (u + 1))
                    for c in range(CH):
                        t = CH * s + c
                        wait(dve, state_step, 8 * u + 2 * c)
                        for a in range(2):
                            rows_a, cols_a = slice(HD * a, HD * (a + 1)), slice(HD * a, HD * (a + 1))
                            new = state[rows_a, (t + 1) % 8, cols_a]
                            if t + 1 == NT:
                                nc.vector.memset(new, 0.0).then_inc(state_step, 1)
                            else:
                                nc.vector.scalar_tensor_tensor(
                                    new, state[rows_a, t % 8, cols_a],
                                    e_cum[rows_a, (c + 1) * P - 1:(c + 1) * P],
                                    ps[4][rows_a, c * P + HD * a:c * P + HD * (a + 1)],
                                    ALU.mult, ALU.add).then_inc(state_step, 1)
                if last_pair(cur) and s >= 1:
                    mixer_variance(s - 1)
                if last_pair(cur) and s + 1 == NS:
                    for j in range(2):
                        mlp_scale(j, j)
                if last_pair(cur) and 1 <= s < NS - 1:
                    center(s - 1)
                if cur:
                    dve.wait_ge(y_psum, u + 1)
                    dve.wait_ge(xT_ready, u + 1)
                    wait(dve, ylo_ready, u)
                    wait(dve, ystats_done, 2 * u)
                    nc.vector.scalar_tensor_tensor(y_raw[:], xT[:], skip_c[:, bass.ds(g, 1)], ps[5][:],
                                                   ALU.mult, ALU.add).then_inc(y_skip, 1)
                    dve.wait_ge(y_skip, u + 1)
                    dve.wait_ge(gate_ready, u + 1)
                    nc.vector.scalar_tensor_tensor(y_raw[:], y_raw[:], 0.5, gate[:], ALU.mult, ALU.mult)\
                        .then_inc(y_ready, 1)
                if last_pair(cur) and s >= 1:
                    if s + 1 == NS:
                        center(s - 1)
                    mixer_rstd(s - 1)
                    if s + 1 < NS:
                        residual(s - 1)
                if nxt:
                    if cur:
                        dve.wait_ge(y_psum, u + 1)
                    decay_args(*nxt)
                if first_pair(nxt) and i is not None and i + 1 < NS:
                    row_stats(i + 1)
                if last_pair(cur) and s == 0:
                    for bank, row in ((6, s1_row), (7, beta_row)):
                        dve.wait_ge(wsums_psum, 1)
                        nc.vector.tensor_copy(row[:], ps[bank][:]).then_inc(wsums_ready, 1)
                if last_pair(cur) and s + 1 == NS:
                    add_beta_row(NS + s - 1)
                    residual(s - 1)
                if last_pair(cur) and 1 <= s < NS - 1:
                    row_stats(NS + s - 1)
                if cur:
                    first = isinstance(g, int) and g == 0
                    add_out(u, s, 0, first)
                    add_out(u, s, 1, first)
                if nxt:
                    n = NS * nxt[0] + nxt[1]
                    dve.wait_ge(tanh_ready, n + 1)
                    nc.vector.scalar_tensor_tensor(gate[:], gate[:], 1.0, ps[1][:], ALU.add, ALU.mult)\
                        .then_inc(gate_ready, 1)
                if cur:
                    add_out(u, s, 2, first)
                    add_out(u, s, 3, first)
                    if s == NS - 1 and not (isinstance(g, int) and g + 1 >= PAIRS):
                        scale_output_weights(g + 1)
                if i is not None and i < NS:
                    cumulate(i)
                if last_pair(cur) and s + 1 == NS:
                    read_mixer_stats(s)
                    mixer_variance(s)
                    row_stats(NS + s - 1)
            mixer(dve, step)

            def mlp_step(cur, nxt):
                if cur:
                    g, s, j = cur
                    v = place(cur)
                    if s == NS - 1 and not (isinstance(g, int) and g + 2 >= HG):
                        dve.wait_ge(gelu_ready, v + 1)
                        mlp_scale(g + 2, j)
                    if first_round(cur):
                        dve.wait_ge(xn_ready, CH * (NS + s + 1))
                        if v == 0:
                            row_rstd(NS + 2)
                            center(3)
                        if v == 1:
                            mixer_rstd(3)
                            residual(3)
                        if v == 2:
                            row_stats(NS + 3)
                        if v == 3:
                            row_rstd(NS + 3)
                    else:
                        dve.wait_ge(acc_set, CH * (s + 1))
                    for c in range(CH):
                        dve.wait_ge(mlp_psum, CH * v + c + 1)
                        row = acc[:, CH * s + c, :]
                        nc.vector.tensor_tensor(row, row, ps[2 + c][:], ALU.add).then_inc(mlp_added, 1)
                    if first_round(cur):
                        if v >= NS:
                            t0 = CH * (v - NS)
                            dve.wait_ge(mlp_added, CH * (v + 1))
                            dve.wait_ge(gb_b2_ready, 1)
                            for t in range(t0, t0 + CH):
                                nc.vector.tensor_tensor(acc[:, t, :], acc[:, t, :], gb_b2[:], ALU.add)\
                                    .then_inc(acc_set, 1)
            mlp(dve, mlp_step)

        @block.tensor
        def _(pe):
            def three(bank, hi_l, lo_l, hi_r, lo_r, start, stop):
                nc.tensor.matmul(bank, lhsT=hi_l, rhs=hi_r, start=start, stop=False)
                nc.tensor.matmul(bank, lhsT=hi_l, rhs=lo_r, start=False, stop=False)
                return nc.tensor.matmul(bank, lhsT=lo_l, rhs=hi_r, start=False, stop=stop)

            def modulation(j):
                pe.wait_ge(wmod_loaded[j % 2], 16 * (j // 2 + 1))
                gate_vector = j % 3 == 2
                wait(pe, modrow_ready, j - 2 if not gate_vector else 0)
                dst = ps[2 + j // 3][:] if gate_vector else ps[j % 3][0:1, :]
                for k in range(KT):
                    ins = nc.tensor.matmul(dst, lhsT=silu_b[:, k, :] if gate_vector else cc[:, 3, k:k + 1],
                                           rhs=w_mod_sb[:, j % 2, k, :], start=k == 0, stop=k == KT - 1)
                ins.then_inc(mod_psum, 1)

            def transpose_rows(i, ks):
                pe.wait_ge(xn_ready, CH * (i + 1))
                for k in ks:
                    if k >= 2:
                        pe.wait_ge(hraw_ready, KT * i + k - 1)
                    for c in range(CH):
                        ins = nc.tensor.transpose(ps[6 + k % 2][:, c * P:(c + 1) * P],
                                                  x_row(i, c)[:, k * P:(k + 1) * P], ident[:])
                    ins.then_inc(xnT_psum, 1)

            def project_decays(i):
                pe.wait_ge(hraw_ready, KT * (i + 1))
                for k in range(KT):
                    ins = nc.tensor.matmul(ps[6][0:HEADS, :], lhsT=w_dec[:, k, :], rhs=h_raw(i, k)[:, :],
                                           start=k == 0, stop=k == KT - 1)
                ins.then_inc(a_psum, 1)

            def decay_columns(i):
                pe.wait_ge(cum_ready, CH * (i + 1))
                pe.wait_ge(wend_ready, i + 1)
                for j, src in enumerate((cum_r, ea)):
                    for c in range(CH):
                        at = j * P + c * HEADS
                        ins = nc.tensor.transpose(ps[7][:, at:at + HEADS], src[:, c * P:(c + 1) * P],
                                                  ident[0:HEADS, 0:HEADS])
                ins.then_inc(cols_psum, 1)

            pe.wait_ge(silu_ready, KT)
            modulation(0)
            modulation(1)
            pe.wait_ge(consts_made, 6)
            transpose_rows(0, range(KT))
            pe.wait_ge(const_loaded, 16 * 6)
            modulation(2)
            project_decays(0)
            modulation(3)
            modulation(4)
            decay_columns(0)
            modulation(5)
            pe.wait_ge(modrow_ready, 4)
            pe.wait_ge(zeroed, 5)

            def project(m, g, s, bank, done):
                if m == B_ and isinstance(g, int) and g == 0:
                    pe.wait_ge(hlo_ready, KT * (s + 1))
                if s == 0:
                    pe.wait_ge(whi_ready[m], g + 1)
                    pe.wait_ge(wlo_ready[m], g + 1)
                tokens = slice(s * SUP, (s + 1) * SUP)
                for k in range(KT):
                    cols = slice(k * P, (k + 1) * P)
                    ins = three(ps[bank][:], w_hi[m][:, cols], w_lo[m][:, cols], hT_hi[:, k, tokens],
                                hT_lo[:, k, tokens], k == 0, k == KT - 1)
                ins.then_inc(done, 1)

            def hidden(unit):
                g, s, j = unit
                if s == 0:
                    pe.wait_ge(whi_ready[j], split_count(g, j))
                    pe.wait_ge(wlo_ready[j], split_count(g, j))
                if first_round(unit):
                    pe.wait_ge(hlo_ready, KT * (NS + s + 1))
                tokens = slice(s * SUP, (s + 1) * SUP)
                for k in range(KT):
                    cols = slice(k * P, (k + 1) * P)
                    ins = three(ps[half(unit)][:], w_hi[j][:, cols], w_lo[j][:, cols], hT_hi[:, k, tokens],
                                hT_lo[:, k, tokens], k == 0, k == KT - 1)
                ins.then_inc(hid_psum, 1)

            def step(cur, nxt):
                i = norm_at(cur, nxt)
                if cur:
                    g, s = cur
                    u = NS * g + s
                    pe.wait_ge(xT_ready, u + 1)
                    wait(pe, state_step, 8 * u)
                    for c in range(CH):
                        part = slice(c * P, (c + 1) * P)
                        ins = nc.tensor.transpose(ps[4][:, part], xT[:, part], ident[:])
                    ins.then_inc(xtok_psum, 1)
                    pe.wait_ge(bT_ready, u + 1)
                    wait(pe, y_skip, u)
                    for c in range(CH):
                        part = slice(c * P, (c + 1) * P)
                        ins = nc.tensor.transpose(ps[5][:, part], bT[:, part], ident[:])
                    ins.then_inc(btok_psum, 1)
                    pe.wait_ge(cT_ready, u + 1)
                    if first_pair(cur) and s == 0:
                        pe.wait_ge(gate_row_ready, 2)
                    for a in range(2):
                        wait(pe, acc_added, CH * u - 3 + a)
                        head = slice(HD * a, HD * (a + 1))
                        for c in range(CH):
                            part = slice(c * P, (c + 1) * P)
                            ins = nc.tensor.matmul(ps[2 + a][:, part], lhsT=bT[head, part], rhs=cT[head, part],
                                                   start=True, stop=True)
                    ins.then_inc(scores_psum, 1)
                if nxt:
                    gn, sn = nxt
                    n = NS * gn + sn
                    wait(pe, xT_ready, n)
                    if last_pair(cur):
                        wait(pe, ystat_read, s)
                    project(B_, gn, sn, 0, bT_psum)
                if first_pair(nxt) and sn:
                    pe.wait_ge(hraw_ready, KT * (sn + 1))
                    wait(pe, acc_added, CH * (n - 1))
                    decay_columns(sn)
                if cur:
                    pe.wait_ge(xtok_ready, u + 1)
                    pe.wait_ge(btok_ready, u + 1)
                    for c in range(CH):
                        ins = nc.tensor.matmul(ps[4][:, c * P:(c + 1) * P], lhsT=b_tok[:, c, :],
                                               rhs=x_tok[:, c, :], start=True, stop=True)
                    ins.then_inc(dstate_psum, 1)
                if last_pair(cur) and s + 1 == NS:
                    pe.wait_ge(ystat_read, s)
                    hidden((0, 0, 0))
                if nxt:
                    wait(pe, gate_ready, n)
                    project(C_, gn, sn, 1, cT_psum)
                if cur:
                    pe.wait_ge(state_step, 8 * (u + 1))
                    pe.wait_ge(cdec_ready, u + 1)
                    for c in range(CH):
                        part = slice(c * P, (c + 1) * P)
                        nc.tensor.matmul(ps[5][:, part], lhsT=state[:, (CH * s + c) % 8, :], rhs=c_dec[:, part],
                                         start=c == 0, stop=False, skip_group_check=True)
                    pe.wait_ge(mixed_ready, 2 * (u + 1))
                    for c in range(CH):
                        part = slice(c * P, (c + 1) * P)
                        for a in range(2):
                            head = slice(HD * a, HD * (a + 1))
                            ins = nc.tensor.matmul(ps[5][head, part], lhsT=x_tok[:, c, head],
                                                   rhs=dec[:, a, part], start=False, stop=True,
                                                   skip_group_check=True)
                    ins.then_inc(y_psum, 1)
                if i is not None:
                    if i < NS:
                        pe.wait_ge(cols_ready, 2 * i)
                        pe.wait_ge(ea_ready, i)
                    if cur:
                        wait(pe, acc_added, CH * u)
                    transpose_rows(i, (0, 1))
                if nxt:
                    pe.wait_ge(bT_ready, n + 1)
                    project(X_, gn, sn, 0, xT_psum)
                if last_pair(cur) and s == 0:
                    pe.wait_ge(wsums_scaled, 2)
                    pe.wait_ge(acc_added, CH * u)
                    nc.tensor.matmul(ps[6][:], lhsT=ones[:], rhs=wg_sum[:], start=True, stop=True)
                    nc.tensor.matmul(ps[7][:], lhsT=ones[:], rhs=wb_sum[:], start=True, stop=True)\
                        .then_inc(wsums_psum, 1)
                if last_pair(cur) and s + 1 == NS:
                    pe.wait_ge(gate_ready, u + 1)
                    hidden((1, 0, 1))
                if i is not None:
                    transpose_rows(i, (2, 3))
                if nxt:
                    pe.wait_ge(cT_ready, n + 1)
                    project(Z_, gn, sn, 1, zT_psum)
                if i is not None and i < NS:
                    project_decays(i)
                if cur:
                    pe.wait_ge(yhi_ready, u + 1)
                    pe.wait_ge(ylo_ready, u + 1)
                    if s == 0:
                        pe.wait_ge(whi_ready[O_], g + 1)
                        pe.wait_ge(wlo_ready[O_], g + 1)
                    for c in range(CH):
                        part = slice(c * P, (c + 1) * P)
                        if c == 2:
                            wait(pe, acc_added, CH * u)
                            if last_pair(cur) and s == 0:
                                pe.wait_ge(wsums_ready, 2)
                            if first_pair(nxt):
                                pe.wait_ge(cols_ready, 2 * (sn + 1))
                            if i is not None:
                                pe.wait_ge(hraw_ready, KT * (i + 1))
                        if c == 3 and i is not None and i < NS:
                            pe.wait_ge(ea_ready, i + 1)
                        three(ps[OUT_BANK[c]][:], y_hi[:, 0, part], y_lo[:, 0, part], w_hi[O_][:], w_lo[O_][:],
                              True, True).then_inc(out_psum, 1)
                if last_pair(cur):
                    if nxt:
                        pe.wait_ge(xT_ready, n + 1)
                    else:
                        pe.wait_ge(y_skip, u + 1)
                    pe.wait_ge(ystats_done, 2 * (u + 1))
                    for c in range(CH):
                        part = slice(s * SUP + c * P, s * SUP + (c + 1) * P)
                        for at, sums in ((4 * c, y_sum), (4 * c + 2, yy_sum)):
                            ins = nc.tensor.matmul(ps[stats_bank(s)][:, at:at + 2], lhsT=sums[:, part], rhs=mean_w[:],
                                                   start=True, stop=True)
                    ins.then_inc(ystat_psum, 1)
            mixer(pe, step)

            def mlp_step(cur, nxt):
                i = mlp_norm_at(nxt)
                if i is not None:
                    pe.wait_ge(hraw_ready, KT * i)
                    transpose_rows(i, (0, 1))
                if nxt and not (first_round(nxt) and nxt[1] == 0):
                    wait(pe, gelu_ready, place(nxt) - 1)
                    hidden(nxt)
                if i is not None:
                    transpose_rows(i, (2, 3))
                if cur:
                    g, s, j = cur
                    v, b = place(cur), half(cur)
                    if s == 0:
                        pe.wait_ge(whi_ready[2 + j], split_count(g, j))
                        pe.wait_ge(wlo_ready[2 + j], split_count(g, j))
                    if first_round(cur) and v == 0:
                        pe.wait_ge(acc_added, CH * NS * PAIRS)
                        pe.wait_ge(state_step, 8 * NS * PAIRS)
                        pe.wait_ge(ystat_read, NS)
                    pe.wait_ge(ghi_ready, v + 1)
                    pe.wait_ge(glo_ready, v + 1)
                    for c in range(CH):
                        part = slice(c * P, (c + 1) * P)
                        wait(pe, mlp_added, CH * (v - 1) + c + 1)
                        three(ps[2 + c][:], y_hi[:, b, part], y_lo[:, b, part], w_hi[2 + j][:],
                              w_lo[2 + j][:], True, True).then_inc(mlp_psum, 1)
            mlp(pe, mlp_step)


_OUT = "out_dram"


def kernel(**inputs):
    import numpy as _np
    import concourse.bacc as _bacc
    from concourse import mybir as _mybir
    from concourse.bass_utils import run_bass_kernel_spmd as _run

    def rows(name, *shape):
        return _np.asarray(inputs[name]).reshape(shape)

    def cols(name):
        return rows(name, -1, P).T

    def ktiles(w, n):
        return w.reshape(-1, n, KT, P).transpose(0, 3, 2, 1)

    w_in = _np.asarray(inputs["L0_attn_W_in"])
    main = ktiles(w_in[:4 * INNER], P).reshape(4, PAIRS, P, KT * P)[[2, 3, 0, 1]].transpose(1, 0, 2, 3)
    laid = {
        "x": rows("L0_attn_x", TOKENS, E),
        "w_pairs": main,
        "w_decay": ktiles(w_in[4 * INNER:], HEADS)[0],
        "w_out": _np.asarray(inputs["L0_attn_W_out"]).T.reshape(PAIRS, P, E),
        "gamma": cols("L0_attn_gamma"),
        "beta": cols("L0_attn_beta"),
        "skip": cols("L0_attn_D"),
        "w1": ktiles(_np.asarray(inputs["L0_ffn_proj1"]), P).reshape(HG, P, KT * P),
        "b1": cols("L0_ffn_proj1_bias"),
        "w2": _np.asarray(inputs["L0_ffn_proj2"]).T.reshape(HG, P, E),
        "b2": rows("L0_ffn_proj2_bias", E),
        "cond": cols("L0_c"),
        "w_mod": rows("L0_wmod", KT, P, 6, E).transpose(2, 1, 0, 3),
    }
    nc = _bacc.Bacc("TRN2", target_bir_lowering=False, num_devices=1)
    arrays, args = {}, {}
    for name, a in laid.items():
        a = _np.ascontiguousarray(a)
        arrays[f"{name}_dram"] = a
        args[name] = nc.dram_tensor(f"{name}_dram", a.shape, _mybir.dt.from_np(a.dtype), kind="ExternalInput").ap()
    args["out"] = nc.dram_tensor(_OUT, (TOKENS, E), F32, kind="ExternalOutput").ap()
    adaln_block(nc, **args)
    r = _run(nc, [arrays], core_ids=[0])
    return r.results[0][_OUT].reshape(1, TOKENS, E)
```
